# Optimizing a Trainium2 kernel written in Bass

```python
import numpy as np
import jax
import jax.numpy as jnp

def _softmax(x, axis=-1):
    return jax.nn.softmax(x, axis=axis)

def _gelu(x):
    return jax.nn.gelu(x, approximate=True)

def _silu(x):
    return jax.nn.silu(x)

def _sigmoid(x):
    return jax.nn.sigmoid(x)

def _layernorm(x, axis=-1, eps=1e-05):
    m = jnp.mean(x, axis=axis, keepdims=True)
    v = jnp.var(x, axis=axis, keepdims=True)
    return (x - m) / jnp.sqrt(v + eps)

def _scatter_add(tgt, idx, src, axis=0):
    return tgt.at[idx].add(src)

def _segment_sum(src, seg, n):
    return jax.ops.segment_sum(src, seg, n)
kernel_name = 'mk_perceiver_d1_seqx_r2_0f4abe'

def setup_inputs(seed: int=0):
    np.random.seed(seed)
    _w = jnp.asarray

    def _rec_inputs():
        import jax
        import jax.numpy as jnp
        _rk = jax.random.key(seed)
        x = 7.22e-05 + 1 * jax.random.normal(jax.random.fold_in(_rk, 1), (16, 64, 512), jnp.float32)
        _lenS = 64 - jax.random.randint(jax.random.fold_in(_rk, 7), (16,), 0, max(1, 64 // 4) + 1, jnp.int32)
        _lenS2 = 512 - jax.random.randint(jax.random.fold_in(_rk, 8), (16,), 0, max(1, 512 // 4) + 1, jnp.int32)
        _ctx_1024P = jax.random.normal(jax.random.fold_in(_rk, 11), (16, 16, 512), jnp.float32)
        _ctx_1024c = jax.random.dirichlet(jax.random.fold_in(_rk, 511), 0.3 * jnp.ones((16,), jnp.float32), (16, 512))
        _ctx_1024t = jnp.einsum('bsk,bkd->bsd', _ctx_1024c, _ctx_1024P)
        _ctx_1024t = _ctx_1024t * jax.lax.rsqrt(jnp.mean(jnp.square(_ctx_1024t)) + 1e-12) * 0.953939
        ctx_1024 = 4.13588e-05 + 0.999923 * (_ctx_1024t + 0.3 * jax.random.normal(jax.random.fold_in(_rk, 611), (16, 512, 512), jnp.float32))
        return (x, ctx_1024)
    x, ctx_1024 = _rec_inputs()

    def _L0_xattn_setup():
        import jax, jax.numpy as jnp
        import numpy as np
        H = 16
        DK = 64
        D_MODEL = 512
        key = jax.random.key(seed)
        ks = jax.random.split(key, 9)
        B, T, D = (4, 1024, D_MODEL)
        scale = 1.0 / np.sqrt(D)
        return {'Q': jax.random.normal(ks[0], (B, T, D), dtype=jnp.float32), 'K': jax.random.normal(ks[1], (B, T, D), dtype=jnp.float32), 'V': jax.random.normal(ks[2], (B, T, D), dtype=jnp.float32), 'Wq': jax.random.normal(ks[3], (D, D), dtype=jnp.float32) * scale, 'bq': jax.random.normal(ks[4], (D,), dtype=jnp.float32) * scale, 'Wk': jax.random.normal(ks[5], (D, D), dtype=jnp.float32) * scale, 'bk': jax.random.normal(ks[6], (D,), dtype=jnp.float32) * scale, 'Wv': jax.random.normal(ks[7], (D, D), dtype=jnp.float32) * scale, 'bv': jax.random.normal(ks[8], (D,), dtype=jnp.float32) * scale}
    _L0_xattn_all = _L0_xattn_setup()
    _L0_xattn_in = {k: v for k, v in _L0_xattn_all.items() if k in ('Wq', 'bq', 'Wk', 'bk', 'Wv', 'bv')}
    del _L0_xattn_all

    def _L0_attn_setup():
        import jax, jax.numpy as jnp
        import numpy as np
        D_MODEL = 512
        D_STATE = 16
        D_CONV = 4
        EXPAND = 2
        D_INNER = D_MODEL * EXPAND
        BATCH = 4
        SEQLEN = 2048

        def _selective_scan(xc, delta, A, B, C, D):
            batch, seqlen, d_inner = xc.shape
            d_state = A.shape[1]

            def step(h, inp):
                x_t, dt, B_t, C_t = inp
                A_disc = jnp.exp(dt[:, :, None] * A[None])
                h = A_disc * h + dt[:, :, None] * B_t[:, None, :] * x_t[:, :, None]
                y_t = jnp.einsum('bds,bs->bd', h, C_t) + D[None, :] * x_t
                return (h, y_t)
            h0 = jnp.zeros((batch, d_inner, d_state), xc.dtype)
            xs = (jnp.swapaxes(xc, 0, 1), jnp.swapaxes(delta, 0, 1), jnp.swapaxes(B, 0, 1), jnp.swapaxes(C, 0, 1))
            _, ys = jax.lax.scan(step, h0, xs)
            return jnp.swapaxes(ys, 0, 1)
        key = jax.random.key(seed)
        ks = jax.random.split(key, 10)
        s = 1.0 / np.sqrt(D_MODEL)
        si = 1.0 / np.sqrt(D_INNER)
        return {'x': jax.random.normal(ks[0], (BATCH, SEQLEN, D_MODEL), jnp.float32), 'x_proj_w': jax.random.normal(ks[1], (D_INNER, D_MODEL), jnp.float32) * s, 'dt_proj_w': jax.random.normal(ks[2], (D_INNER, D_MODEL), jnp.float32) * s, 'dt_proj_b': jax.random.normal(ks[3], (D_INNER,), jnp.float32) * 0.1, 'A_log': jax.random.normal(ks[4], (D_INNER, D_STATE), jnp.float32), 'D': jnp.ones((D_INNER,), jnp.float32), 'B_proj_w': jax.random.normal(ks[5], (D_STATE, D_MODEL), jnp.float32) * s, 'C_proj_w': jax.random.normal(ks[6], (D_STATE, D_MODEL), jnp.float32) * s, 'conv_w': jax.random.normal(ks[7], (D_INNER, 1, D_CONV), jnp.float32) * 0.5, 'conv_b': jax.random.normal(ks[8], (D_INNER,), jnp.float32) * 0.1, 'out_proj_w': jax.random.normal(ks[9], (D_MODEL, D_INNER), jnp.float32) * si}
    _L0_attn_all = _L0_attn_setup()
    _L0_attn_in = {k: v for k, v in _L0_attn_all.items() if k in ('x_proj_w', 'dt_proj_w', 'dt_proj_b', 'A_log', 'D', 'B_proj_w', 'C_proj_w', 'conv_w', 'conv_b', 'out_proj_w')}
    del _L0_attn_all

    def _L0_ffn_setup():
        import jax, jax.numpy as jnp
        import numpy as np
        TOP_K = 4
        N_GROUP = 4
        TOPK_GROUP = 2
        ROUTED_SCALING = 1.0

        def _route(x_flat, gate_weight, e_bias):
            T = x_flat.shape[0]
            E = gate_weight.shape[0]
            logits = jnp.einsum('th,eh->te', x_flat, gate_weight)
            scores = jax.nn.sigmoid(logits)
            scores_for_choice = scores + e_bias[None, :]
            grp = scores_for_choice.reshape(T, N_GROUP, E // N_GROUP)
            top2, _ = jax.lax.top_k(grp, 2)
            group_scores = top2.sum(axis=-1)
            _, group_idx = jax.lax.top_k(group_scores, TOPK_GROUP)
            group_mask = jax.nn.one_hot(group_idx, N_GROUP, dtype=scores.dtype).sum(axis=1)
            score_mask = jnp.repeat(group_mask, E // N_GROUP, axis=1)
            tmp_scores = jnp.where(score_mask > 0, scores_for_choice, 0.0)
            _, topk_idx = jax.lax.top_k(tmp_scores, TOP_K)
            topk_weight = jnp.take_along_axis(scores, topk_idx, axis=1)
            denom = topk_weight.sum(axis=-1, keepdims=True) + 1e-20
            topk_weight = topk_weight / denom * ROUTED_SCALING
            return (topk_idx, topk_weight)
        key = jax.random.key(seed)
        k1, k2, k3, k4, k5 = jax.random.split(key, 5)
        B, S, H, I, E = (1, 1024, 512, 256, 16)
        hidden_states = jax.random.normal(k1, (B, S, H), dtype=jnp.float32)
        gate_weight = jax.random.normal(k2, (E, H), dtype=jnp.float32) * (1.0 / np.sqrt(H))
        e_bias = jnp.zeros((E,), dtype=jnp.float32)
        gate_proj = jax.random.normal(k3, (E, I, H), dtype=jnp.float32) * 0.02
        up_proj = jax.random.normal(k4, (E, I, H), dtype=jnp.float32) * 0.02
        down_proj = jax.random.normal(k5, (E, H, I), dtype=jnp.float32) * 0.02
        return {'hidden_states': hidden_states, 'gate_weight': gate_weight, 'e_bias': e_bias, 'gate_proj': gate_proj, 'up_proj': up_proj, 'down_proj': down_proj}
    _L0_ffn_all = _L0_ffn_setup()
    _L0_ffn_in = {k: v for k, v in _L0_ffn_all.items() if k in ('gate_weight', 'e_bias', 'gate_proj', 'up_proj', 'down_proj')}
    del _L0_ffn_all
    return {'x': x, 'ctx_1024': ctx_1024, 'L0_xattn_Wq': _L0_xattn_in['Wq'], 'L0_xattn_bq': _L0_xattn_in['bq'], 'L0_xattn_Wk': _L0_xattn_in['Wk'], 'L0_xattn_bk': _L0_xattn_in['bk'], 'L0_xattn_Wv': _L0_xattn_in['Wv'], 'L0_xattn_bv': _L0_xattn_in['bv'], 'L0_attn_x_proj_w': _L0_attn_in['x_proj_w'], 'L0_attn_dt_proj_w': _L0_attn_in['dt_proj_w'], 'L0_attn_dt_proj_b': _L0_attn_in['dt_proj_b'], 'L0_attn_A_log': _L0_attn_in['A_log'], 'L0_attn_D': _L0_attn_in['D'], 'L0_attn_B_proj_w': _L0_attn_in['B_proj_w'], 'L0_attn_C_proj_w': _L0_attn_in['C_proj_w'], 'L0_attn_conv_w': _L0_attn_in['conv_w'], 'L0_attn_conv_b': _L0_attn_in['conv_b'], 'L0_attn_out_proj_w': _L0_attn_in['out_proj_w'], 'L0_ffn_gate_weight': _L0_ffn_in['gate_weight'], 'L0_ffn_e_bias': _L0_ffn_in['e_bias'], 'L0_ffn_gate_proj': _L0_ffn_in['gate_proj'], 'L0_ffn_up_proj': _L0_ffn_in['up_proj'], 'L0_ffn_down_proj': _L0_ffn_in['down_proj']}

def reference(x, ctx_1024, L0_xattn_Wq, L0_xattn_bq, L0_xattn_Wk, L0_xattn_bk, L0_xattn_Wv, L0_xattn_bv, L0_attn_x_proj_w, L0_attn_dt_proj_w, L0_attn_dt_proj_b, L0_attn_A_log, L0_attn_D, L0_attn_B_proj_w, L0_attn_C_proj_w, L0_attn_conv_w, L0_attn_conv_b, L0_attn_out_proj_w, L0_ffn_gate_weight, L0_ffn_e_bias, L0_ffn_gate_proj, L0_ffn_up_proj, L0_ffn_down_proj):
    import jax
    import jax.numpy as jnp

    def _L0_xattn_ref(Q, K, V, Wq, bq, Wk, bk, Wv, bv):
        import jax, jax.numpy as jnp
        import numpy as np
        H = 16
        DK = 64
        D_MODEL = 512
        B = Q.shape[0]

        def proj(x, W, b):
            y = jnp.einsum('btd,ed->bte', x, W) + b
            return y.reshape(B, -1, H, DK).transpose(0, 2, 1, 3)
        q = proj(Q, Wq, bq)
        k = proj(K, Wk, bk)
        v = proj(V, Wv, bv)
        scores = jnp.einsum('bhqd,bhkd->bhqk', q, k) / jnp.sqrt(jnp.float32(DK))
        attn = jax.nn.softmax(scores, axis=-1)
        out = jnp.einsum('bhqk,bhkd->bhqd', attn, v)
        return out.transpose(0, 2, 1, 3).reshape(B, -1, D_MODEL)

    def _L0_attn_ref(x, x_proj_w, dt_proj_w, dt_proj_b, A_log, D, B_proj_w, C_proj_w, conv_w, conv_b, out_proj_w):
        import jax, jax.numpy as jnp
        import numpy as np
        D_MODEL = 512
        D_STATE = 16
        D_CONV = 4
        EXPAND = 2
        D_INNER = D_MODEL * EXPAND
        BATCH = 4
        SEQLEN = 2048

        def _selective_scan(xc, delta, A, B, C, D):
            batch, seqlen, d_inner = xc.shape
            d_state = A.shape[1]

            def step(h, inp):
                x_t, dt, B_t, C_t = inp
                A_disc = jnp.exp(dt[:, :, None] * A[None])
                h = A_disc * h + dt[:, :, None] * B_t[:, None, :] * x_t[:, :, None]
                y_t = jnp.einsum('bds,bs->bd', h, C_t) + D[None, :] * x_t
                return (h, y_t)
            h0 = jnp.zeros((batch, d_inner, d_state), xc.dtype)
            xs = (jnp.swapaxes(xc, 0, 1), jnp.swapaxes(delta, 0, 1), jnp.swapaxes(B, 0, 1), jnp.swapaxes(C, 0, 1))
            _, ys = jax.lax.scan(step, h0, xs)
            return jnp.swapaxes(ys, 0, 1)
        seqlen = x.shape[1]
        x_inner = x @ x_proj_w.T
        xc = jax.lax.conv_general_dilated(jnp.swapaxes(x_inner, 1, 2), conv_w, window_strides=(1,), padding=[(D_CONV - 1, 0)], dimension_numbers=('NCH', 'OIH', 'NCH'), feature_group_count=D_INNER)
        xc = jnp.swapaxes(xc + conv_b[None, :, None], 1, 2)
        xc = jax.nn.silu(xc)
        B = x @ B_proj_w.T
        C = x @ C_proj_w.T
        delta = jax.nn.softplus(x @ dt_proj_w.T + dt_proj_b)
        A = -jnp.exp(A_log.astype(jnp.float32))
        y = _selective_scan(xc, delta, A, B, C, D)
        return y @ out_proj_w.T

    def _L0_ffn_ref(hidden_states, gate_weight, e_bias, gate_proj, up_proj, down_proj):
        import jax, jax.numpy as jnp
        import numpy as np
        TOP_K = 4
        N_GROUP = 4
        TOPK_GROUP = 2
        ROUTED_SCALING = 1.0

        def _route(x_flat, gate_weight, e_bias):
            T = x_flat.shape[0]
            E = gate_weight.shape[0]
            logits = jnp.einsum('th,eh->te', x_flat, gate_weight)
            scores = jax.nn.sigmoid(logits)
            scores_for_choice = scores + e_bias[None, :]
            grp = scores_for_choice.reshape(T, N_GROUP, E // N_GROUP)
            top2, _ = jax.lax.top_k(grp, 2)
            group_scores = top2.sum(axis=-1)
            _, group_idx = jax.lax.top_k(group_scores, TOPK_GROUP)
            group_mask = jax.nn.one_hot(group_idx, N_GROUP, dtype=scores.dtype).sum(axis=1)
            score_mask = jnp.repeat(group_mask, E // N_GROUP, axis=1)
            tmp_scores = jnp.where(score_mask > 0, scores_for_choice, 0.0)
            _, topk_idx = jax.lax.top_k(tmp_scores, TOP_K)
            topk_weight = jnp.take_along_axis(scores, topk_idx, axis=1)
            denom = topk_weight.sum(axis=-1, keepdims=True) + 1e-20
            topk_weight = topk_weight / denom * ROUTED_SCALING
            return (topk_idx, topk_weight)
        B, S, H = hidden_states.shape
        E = gate_proj.shape[0]
        x = hidden_states.reshape(-1, H).astype(jnp.float32)
        topk_idx, topk_weight = _route(x, gate_weight, e_bias)
        combine = (jax.nn.one_hot(topk_idx, E, dtype=x.dtype) * topk_weight[..., None]).sum(axis=1)
        g = jnp.einsum('th,eih->tei', x, gate_proj)
        u = jnp.einsum('th,eih->tei', x, up_proj)
        act = jax.nn.silu(g) * u
        expert_out = jnp.einsum('tei,ehi->teh', act, down_proj)
        y = jnp.einsum('teh,te->th', expert_out, combine)
        return y.reshape(B, S, H)
    x = x + _L0_xattn_ref(_layernorm(x, axis=-1), ctx_1024, ctx_1024, L0_xattn_Wq, L0_xattn_bq, L0_xattn_Wk, L0_xattn_bk, L0_xattn_Wv, L0_xattn_bv)
    x = x + _L0_attn_ref(_layernorm(x, axis=-1), L0_attn_x_proj_w, L0_attn_dt_proj_w, L0_attn_dt_proj_b, L0_attn_A_log, L0_attn_D, L0_attn_B_proj_w, L0_attn_C_proj_w, L0_attn_conv_w, L0_attn_conv_b, L0_attn_out_proj_w)
    x = x + _L0_ffn_ref(_layernorm(x, axis=-1), L0_ffn_gate_weight, L0_ffn_e_bias, L0_ffn_gate_proj, L0_ffn_up_proj, L0_ffn_down_proj)
    return x

_drawn_inputs = setup_inputs


def setup_inputs(seed=0):
    import zlib

    import numpy as np

    out = dict(_drawn_inputs(seed))
    spreads = {'L0_attn_D': (1.0, 0.2), 'L0_ffn_e_bias': (0.0, 0.8)}
    factors = {'L0_xattn_bq': 3.773,
     'L0_xattn_bk': 8.0,
     'L0_ffn_gate_weight': 8.0,
     'L0_ffn_gate_proj': 8.0,
     'L0_ffn_up_proj': 8.0,
     'L0_ffn_down_proj': 8.0}
    for name, (base, spread) in spreads.items():
        noise = np.random.default_rng([zlib.crc32(name.encode()), seed]).standard_normal(out[name].shape)
        drawn = base * np.exp(spread * noise) if base else spread * noise
        out[name] = jnp.asarray(drawn.astype(out[name].dtype))
    for name, factor in factors.items():
        out[name] = (out[name] * factor).astype(out[name].dtype)
    return out
```

```python
from contextlib import ExitStack

import concourse.bass as bass
from concourse import mybir

ALU = mybir.AluOpType
ACT = mybir.ActivationFunctionType
F32 = mybir.dt.float32
AX_X = mybir.AxisListType.X

P = 128
D = 512
DC = D // P
T = 64
NB = 16
S_CTX = 512
KEYS = S_CTX // 2
KC = KEYS // P
G = 2
GB = NB // G
GT = GB * T
NT = GT // P
SUBS = 2
SB = GB // SUBS
ST = SB * T
NU = 2 * SB
TI = T // 2
H = 8
DH = D // H
Q = H * TI
QB = Q // P
DI = 1024
NBK = DI // P
NS = 16
HALF = NBK // 2
SW = HALF * GT
TAPS = 4
E = 16
TOPK = 4
I = 256
IC = I // P
NG = 4
EPS = 1e-5
RESET = 1e30

C_BQ = 0
C_BV = C_BQ + DC
C_DTB = C_BV + DC
C_CW = C_DTB + NBK
C_CB = C_CW + NBK * TAPS
C_D = C_CB + NBK
C_A = C_D + NBK
C_BK = C_A + NBK * NS
C_EB = C_BK + DC * H
C_T4 = C_EB + E
C_T16 = C_T4 + NG * NG
C_ID = C_T16 + E * E
C_END = C_ID + P


def perceiver_block(nc, x, ctx_t, ctx_n, wq_t, wk, wv_t, xp_t, dt_t, bc_t, ow_t, gate_t,
                    eg_t, eu_t, ed_t, params, bc_dram, comb_dram, out):
    with ExitStack() as es:
        def sb(name, cols):
            return es.enter_context(nc.sbuf_tensor(name, [P, cols], F32))

        def sem(name):
            return es.enter_context(nc.semaphore(name))

        xs_ = sb("x_tokens", G * NT * D)
        xs = xs_[:, :].rearrange("p (n d) -> p n d", d=D)
        nrm_ = sb("normed", NT * D)
        nrm = nrm_[:, :].rearrange("p (n d) -> p n d", d=D)
        sb8 = nrm_[0:H, 0:NU * Q].rearrange("p (u h i) -> p u h i", u=NU, h=H)
        bcT = nrm_[0:2 * NS, 0:GT]
        combT = nrm_[0:E, 0:GT]
        xT_ = sb("normed_t", DC * GT)
        xT = xT_[:, :].rearrange("p (c t) -> p c t", c=DC)
        qT_ = sb("q_t", DC * ST)
        qT = qT_[:, :].rearrange("p (m t) -> p m t", m=DC)
        QT_ = sb("queries_ctx", NU * DC * Q)
        QT = QT_[:, :].rearrange("p (u c q) -> p u c q", u=NU, c=DC)
        ctx_ = sb("ctx", 2 * (DC * KEYS + KC * D))
        ctxT = [ctx_[:, s * 2048:s * 2048 + 1024].rearrange("p (c k) -> p c k", c=DC) for s in range(2)]
        ctxN = [ctx_[:, s * 2048 + 1024:s * 2048 + 2048].rearrange("p (j d) -> p j d", j=KC) for s in range(2)]
        ow = ctx_[:, :].rearrange("p (k d) -> p k d", k=NBK)
        pp_ = sb("probs", 4 * QB * KEYS)
        prob = [pp_[:, s * 512:(s + 1) * 512].rearrange("p (b k) -> p b k", b=QB) for s in range(2)]
        probT = [pp_[:, 1024 + s * 512:1536 + s * 512].rearrange("p (j q) -> p j q", j=KC) for s in range(2)]
        rk1 = pp_[:, 0:1024]
        rk2 = pp_[:, 1024:2048]
        w_ = sb("attn_weights", 3 * DC * D)
        wq, wkt, wv = (w_[:, k * 2048:(k + 1) * 2048].rearrange("p (c d) -> p c d", c=DC) for k in range(3))
        xTm = w_[:, 0:2048].rearrange("p (c t) -> p c t", c=DC)
        th = [w_[:, 2048 + s * 512:2560 + s * 512] for s in range(2)]
        hb = [w_[:, 3072 + s * 512:3584 + s * 512] for s in range(2)]
        hc = [w_[:, 4096 + s * 512:4608 + s * 512] for s in range(2)]
        cb = [w_[:, 5120 + s * 512:5632 + s * 512] for s in range(2)]
        MW = 2 * DC * I + IC * D
        eg = [QT_[:, s * MW:s * MW + 1024].rearrange("p (c i) -> p c i", c=DC) for s in range(2)]
        eu = [QT_[:, s * MW + 1024:s * MW + 2048].rearrange("p (c i) -> p c i", c=DC) for s in range(2)]
        ed = [QT_[:, s * MW + 2048:s * MW + 3072].rearrange("p (c d) -> p c d", c=IC) for s in range(2)]
        r_ = sb("scan_scratch", 4 * SW)
        dA = [r_[:, s * SW:(s + 1) * SW] for s in range(2)]
        hs = [r_[:, (2 + s) * SW:(3 + s) * SW] for s in range(2)]
        xp = r_[:, 0:4096].rearrange("p (c n) -> p c n", c=DC)
        dtw = r_[:, 4096:8192].rearrange("p (c n) -> p c n", c=DC)
        acc_ = sb("y_acc", NBK * GT)
        del_ = sb("delta", NBK * GT)
        u_ = sb("u", NBK * GT)
        acc, dlt, u = (a[:, :].rearrange("p (k t) -> p k t", k=NBK) for a in (acc_, del_, u_))
        bcs_ = sb("bc_bcast", 4 * GT)
        bcs = [bcs_[:, s * 1024:(s + 1) * 1024].rearrange("p (w t) -> p w t", w=2) for s in range(2)]
        XP = GB * (T + TAPS - 1)
        xi = [bcs_[:, s * XP:(s + 1) * XP].rearrange("p (b t) -> p b t", b=GB) for s in range(2)]
        par = sb("params", C_END)
        bcw_ = sb("bc_weights", DC * 2 * NS)
        bcw = bcw_[:, :].rearrange("p (c n) -> p c n", c=DC)
        gwt_ = sb("gate_weights", DC * E)
        gwt = gwt_[:, :].rearrange("p (c n) -> p c n", c=DC)
        ident = par[:, C_ID:C_ID + P]
        st_ = sb("stats", 6 * NT)
        mv_ = sb("mean_var", 2 * NT)
        mv = mv_[:, :].rearrange("p (n k) -> p n k", k=2)
        rstd = sb("rstd", NT)
        nmax = sb("neg_max", 2 * QB)
        rsum = sb("row_sum", 2 * QB)
        lg, sc, sfc, gs = (nrm_[:, 1024 + k * NT * E:1024 + (k + 1) * NT * E] for k in range(4))
        ones8 = sb("ones", 1)
        epsc = sb("eps", 1)

        bank = [es.enter_context(nc.psum_tensor(f"bank{i}", [P, 512], F32)) for i in range(8)]

        x_in = sem("x_in")
        par_in = sem("par_in")
        sw_in = sem("small_w_in")
        wq_in = sem("wq_in")
        ctxT_in = [sem(f"ctx_t_in{s}") for s in range(2)]
        ctxN_in = [sem(f"ctx_n_in{s}") for s in range(2)]
        pw_in = sem("proj_w_in")
        ow_in = sem("out_w_in")
        ew_in = [sem(f"expert_w_in{s}") for s in range(2)]
        cb_in = [sem(f"comb_in{s}") for s in range(2)]
        bc_in = [sem(f"bc_in{s}") for s in range(2)]
        bc_out = sem("bc_written")
        comb_out = sem("comb_written")
        out_done = sem("out_done")
        act_step = sem("act_step")
        act_bc = sem("bc_ready")
        comb_act = sem("comb_t_ready")
        dve_step = sem("dve_step")
        negA_rdy = sem("negA_ready")
        aexp = sem("a_exp")
        ones_rdy = sem("ones_ready")
        var_rdy = sem("var_ready")
        std_rdy = sem("std_ready")
        nrm_rdy = sem("norm_ready")
        a_full = sem("bankA_full")
        a_free = sem("bankA_free")
        d_full = sem("bankD_full")
        d_free = sem("bankD_free")
        sb8_rdy = sem("qbk_ready")
        s_full = sem("scores_full")
        nm_rdy = sem("neg_max_ready")
        p_exp = sem("probs_exp")
        p_nrm = sem("probs_normed")
        t_full = sem("probsT_full")
        t_copied = sem("probsT_copied")
        x1_rdy = sem("attn_added")
        sp_rdy = sem("softplus_ready")
        conv_done = sem("conv_done")
        xi_rdy = sem("xi_ready")
        tanh_rdy = sem("tanh_ready")
        sp_used = sem("softplus_used")
        pad_rdy = sem("xi_pads_ready")
        dl_rdy = sem("delta_ready")
        cv_all = sem("conv_all")
        da_rdy = sem("dA_ready")
        scan_rd = sem("scan_read")
        step_done = sem("scan_step_done")
        logit_e = sem("logit_exp")
        comb_rdy = sem("comb_ready")
        gu_full = sem("gate_up_full")
        th_rdy = sem("tanh_gate_ready")
        hb_rdy = sem("hidden_ready")
        hc_rdy = sem("hidden_weighted")
        dn_done = sem("down_done")
        y_read = sem("y_read")

        ATTN_A = DC + DC * DC + DC
        PROJ_A = 1 + 2 * NBK
        PROJ_JOBS = [DC + 2 * ATTN_A + DC + 1 + NBK, 0]
        ROUTE_JOBS = [DC + 2 * ATTN_A + DC + PROJ_A + DC + 2 * ATTN_A + DC + 1, 0]
        PROJ_JOBS[1] = ROUTE_JOBS[0] + 1 + DC + 1 + NBK
        ROUTE_JOBS[1] = ROUTE_JOBS[0] + 1 + DC + PROJ_A + DC + 1

        class Count:
            n = 0

        def unit(sg, k):
            return sg * NU + k

        def ctx_read(n):
            return (n // NU) * (1 + 2 * NU + ST // P) + 1 + 2 * (n % NU + 1)

        steps_per_group = 2 * NS

        block = es.enter_context(nc.Block())

        @block.sync
        def _(sp):
            def load_ctx_t(n):
                if n < 4 * NU:
                    if n >= 2:
                        sp.wait_ge(s_full, n - 1)
                    sp.dma_start(ctxT[n % 2], ctx_t[n // 2, n % 2].rearrange("(c p) k -> p c k", p=P))\
                      .then_inc(ctxT_in[n % 2], 16)

            def load_ctx_n(n):
                if n >= 2:
                    sp.wait_ge(d_full, ctx_read(n - 2))
                rows = ctx_n[n // 2].rearrange("(j p two) d -> two p j d", p=P, two=2)
                sp.dma_start(ctxN[n % 2], rows[n % 2]).then_inc(ctxN_in[n % 2], 16)

            def load_proj():
                sp.dma_start(xp, xp_t.rearrange("(c p) n -> p c n", p=P)).then_inc(pw_in, 16)
                sp.dma_start(dtw, dt_t.rearrange("(c p) n -> p c n", p=P)).then_inc(pw_in, 16)

            def store_bc(g):
                sp.wait_ge(act_bc, g + 1)
                sp.dma_start(bc_dram[g], bcT).then_inc(bc_out, 16)

            def load_bc(g, s):
                k = g * NS + s
                if s == 0:
                    sp.wait_ge(bc_out, 16 * (g + 1))
                    sp.wait_ge(cv_all, g + 1)
                if s >= 2:
                    sp.wait_ge(step_done, 2 * (k - 1))
                src = bc_dram[g].rearrange("(w s) t -> s w t", w=2)[s]
                sp.dma_start(bcs[s % 2], src.unsqueeze(0).to_broadcast([P, 2, GT])).then_inc(bc_in[s % 2], 16)

            def load_expert(g, e):
                k = g * E + e
                if k == 0:
                    sp.wait_ge(x1_rdy, NT * G)
                if k >= 2:
                    sp.wait_ge(dn_done, IC * (k - 1))
                sp.dma_start(eg[k % 2], eg_t[e].rearrange("(c p) i -> p c i", p=P)).then_inc(ew_in[k % 2], 16)
                sp.dma_start(eu[k % 2], eu_t[e].rearrange("(c p) i -> p c i", p=P)).then_inc(ew_in[k % 2], 16)
                sp.dma_start(ed[k % 2], ed_t[e].rearrange("(c p) d -> p c d", p=P)).then_inc(ew_in[k % 2], 16)

            def store_comb(g):
                sp.wait_ge(comb_act, g + 1)
                sp.dma_start(comb_dram[g], combT).then_inc(comb_out, 16)

            def load_comb(g, e):
                k = g * E + e
                if e == 0:
                    sp.wait_ge(comb_out, 16 * (g + 1))
                if k >= 2:
                    sp.wait_ge(hc_rdy, IC * (k - 1))
                src = comb_dram[g][e]
                sp.dma_start(cb[k % 2], src.unsqueeze(0).to_broadcast([P, GT])).then_inc(cb_in[k % 2], 16)

            sp.dma_start(par[:, :], params).then_inc(par_in, 16)
            sp.dma_start(xs, x.rearrange("(n p) d -> p n d", p=P)).then_inc(x_in, 16)
            sp.dma_start(wq, wq_t.rearrange("(c p) e -> p c e", p=P)).then_inc(wq_in, 16)
            sp.dma_start(wkt, wk.rearrange("(c p) e -> p c e", p=P)).then_inc(wq_in, 16)
            load_ctx_t(0)
            load_ctx_t(1)
            load_ctx_n(0)
            sp.dma_start(wv, wv_t.rearrange("(c p) e -> p c e", p=P)).then_inc(wq_in, 16)
            sp.dma_start(bcw, bc_t.rearrange("(c p) e -> p c e", p=P)).then_inc(sw_in, 16)
            sp.dma_start(gwt, gate_t.rearrange("(c p) e -> p c e", p=P)).then_inc(sw_in, 16)
            load_proj()
            for n in range(1, 2 * NU):
                load_ctx_t(n + 1)
                load_ctx_n(n)
            store_bc(0)
            load_bc(0, 0)
            load_bc(0, 1)
            for s in range(NS):
                if s + 2 < NS:
                    load_bc(0, s + 2)
                load_ctx_t(2 * NU + s + 1)
                load_ctx_n(2 * NU + s)
            sp.wait_ge(d_full, ctx_read(4 * NU - 1))
            sp.dma_start(ow, ow_t.rearrange("(k p) d -> p k d", p=P)).then_inc(ow_in, 16)
            sp.wait_ge(step_done, steps_per_group)
            load_proj()
            load_expert(0, 0)
            load_expert(0, 1)
            store_comb(0)
            store_bc(1)
            load_comb(0, 0)
            load_comb(0, 1)
            load_bc(1, 0)
            load_bc(1, 1)
            for e in range(E):
                load_expert((e + 2) // E, (e + 2) % E)
                if e + 2 < E:
                    load_comb(0, e + 2)
                    load_bc(1, e + 2)
            def store_out(g):
                sp.wait_ge(y_read, NT * (g + 1))
                sp.dma_start(out[g * GT:(g + 1) * GT].rearrange("(n p) d -> p n d", p=P),
                             xs[:, g * NT:(g + 1) * NT, :]).then_inc(out_done, 16)
            store_out(0)
            store_comb(1)
            load_comb(1, 0)
            load_comb(1, 1)
            for e in range(2, E):
                load_expert(1, e)
                load_comb(1, e)
            store_out(1)
            sp.wait_ge(out_done, 32)

        @block.tensor
        def _(pe):
            ja, jd = Count(), Count()

            def job_a():
                if ja.n >= 2:
                    pe.wait_ge(a_free, ja.n - 1)
                ja.n += 1
                return bank[6 + (ja.n - 1) % 2]

            def job_d():
                if jd.n >= 2:
                    pe.wait_ge(d_free, jd.n - 1)
                jd.n += 1
                return bank[4 + (jd.n - 1) % 2]

            norms = Count()

            def norm_transposes():
                norms.n += 1
                pe.wait_ge(nrm_rdy, norms.n)
                for c in range(DC):
                    b = job_a()
                    for t in range(NT):
                        mm = pe.transpose(b[:, t * P:(t + 1) * P], nrm[:, t, c * P:(c + 1) * P], ident)
                    mm.then_inc(a_full, 1)

            def attn_prep(sg):
                o = (sg % SUBS) * ST
                if sg == 0:
                    pe.wait_ge(wq_in, 48)
                pe.wait_ge(a_free, ja.n)
                for m in range(DC):
                    b = job_a()
                    for c in range(DC):
                        mm = pe.matmul(b[:, 0:ST], wq[:, c, m * P:(m + 1) * P], xT[:, c, o:o + ST],
                                       start=(c == 0), stop=(c == DC - 1))
                    mm.then_inc(a_full, 1)
                pe.wait_ge(a_free, ja.n)
                b = job_d()
                for m in range(DC):
                    mm = pe.matmul(b[0:H, 0:ST], par[:, C_BK + m * H:C_BK + (m + 1) * H], qT[:, m, :],
                                   start=(m == 0), stop=(m == DC - 1))
                mm.then_inc(d_full, 1)
                for c in range(DC):
                    for mp in range(DC // 2):
                        pair = [job_a(), job_a()]
                        for k in range(2):
                            m = 2 * mp + k
                            for hh in range(2):
                                r = slice(hh * DH, (hh + 1) * DH)
                                mm = pe.matmul(pair[hh][:, k * ST:(k + 1) * ST], wkt[r, m, c * P:(c + 1) * P],
                                               qT[r, m, :], start=True, stop=True)
                                if k == 1:
                                    mm.then_inc(a_full, 1)
                pe.wait_ge(a_free, ja.n)
                pe.wait_ge(sb8_rdy, sg + 1)

            def scores(sg, k):
                n = unit(sg, k)
                pe.wait_ge(ctxT_in[n % 2], 16 * (n // 2 + 1))
                if n >= 2:
                    pe.wait_ge(p_exp, n - 1)
                for qb in range(QB):
                    o = bank[n % 2][:, qb * KEYS:(qb + 1) * KEYS]
                    for c in range(DC):
                        pe.matmul(o, QT[:, k, c, qb * P:(qb + 1) * P], ctxT[n % 2][:, c, :], start=(c == 0), stop=False)
                    mm = pe.matmul(o, sb8[:, k, qb * 4:(qb + 1) * 4, :], ones8[0:H, :].to_broadcast([H, KEYS]), start=False, stop=True)
                mm.then_inc(s_full, 1)

            def probs_t(sg, k):
                n = unit(sg, k)
                pe.wait_ge(p_nrm, n + 1)
                if n >= 2:
                    pe.wait_ge(t_copied, n - 1)
                for j in range(KC):
                    for qb in range(QB):
                        mm = pe.transpose(bank[2 + n % 2][:, j * Q + qb * P:j * Q + (qb + 1) * P],
                                          prob[n % 2][:, qb, j * P:(j + 1) * P], ident)
                mm.then_inc(t_full, 1)

            def weighted_ctx(sg, k):
                n = unit(sg, k)
                pe.wait_ge(t_copied, n + 1)
                pe.wait_ge(ctxN_in[n % 2], 16 * (n // 2 + 1))
                for half in range(2):
                    b = job_d()
                    for cc in range(2):
                        c = 2 * half + cc
                        for j in range(KC):
                            mm = pe.matmul(b[:, cc * Q:(cc + 1) * Q], ctxN[n % 2][:, j, c * P:(c + 1) * P],
                                           probT[n % 2][:, j, :], start=(j == 0), stop=(j == KC - 1))
                    mm.then_inc(d_full, 1)

            def attn_units_start(sg):
                scores(sg, 0)

            def attn_unit(sg, k):
                if k + 1 < NU:
                    scores(sg, k + 1)
                if k >= 1:
                    weighted_ctx(sg, k - 1)
                probs_t(sg, k)

            def attn_end(sg):
                weighted_ctx(sg, NU - 1)
                pe.wait_ge(d_free, jd.n)
                for m in range(DC):
                    b = job_a()
                    for hh in range(2):
                        h = 2 * m + hh
                        for c in range(DC):
                            mm = pe.matmul(b[hh * DH:(hh + 1) * DH, 0:ST], wv[:, c, h * DH:(h + 1) * DH],
                                           QT[:, :, c, h * TI:(h + 1) * TI], start=(c == 0), stop=(c == DC - 1))
                    mm.then_inc(a_full, 1)
                pe.wait_ge(a_free, ja.n)
                for t in range(ST // P):
                    b = job_d()
                    for m in range(DC):
                        mm = pe.transpose(b[:, m * P:(m + 1) * P], qT[:, m, t * P:(t + 1) * P], ident)
                    mm.then_inc(d_full, 1)

            def projections(g):
                pe.wait_ge(a_free, ja.n)
                b = job_a()
                for c in range(DC):
                    mm = pe.matmul(b[0:2 * NS, :], bcw[:, c, :], xT[:, c, :], start=(c == 0), stop=(c == DC - 1))
                mm.then_inc(a_full, 1)
                pe.wait_ge(pw_in, 32 * (g + 1))
                for w in (dtw, xp):
                    for k in range(NBK):
                        b = job_a()
                        for c in range(DC):
                            mm = pe.matmul(b[:, :], w[:, c, k * P:(k + 1) * P], xT[:, c, :],
                                           start=(c == 0), stop=(c == DC - 1))
                        mm.then_inc(a_full, 1)

            def out_proj(g):
                pe.wait_ge(step_done, steps_per_group * (g + 1))
                if g == 0:
                    pe.wait_ge(ow_in, 16)
                else:
                    pe.wait_ge(y_read, 4)
                for t in range(NT):
                    b = job_d()
                    for k in range(NBK):
                        mm = pe.matmul(b[:, :], acc[:, k, t * P:(t + 1) * P], ow[:, k, :],
                                       start=(k == 0), stop=(k == NBK - 1))
                    mm.then_inc(d_full, 1)

            def route(g):
                pe.wait_ge(a_free, ja.n)
                b = job_a()
                for t in range(NT):
                    for c in range(DC):
                        mm = pe.matmul(b[:, t * E:(t + 1) * E], xTm[:, c, t * P:(t + 1) * P], gwt[:, c, :],
                                       start=(c == 0), stop=(c == DC - 1))
                mm.then_inc(a_full, 1)
                pe.wait_ge(comb_rdy, g + 1)
                b = job_a()
                for t in range(NT):
                    mm = pe.transpose(b[0:E, t * P:(t + 1) * P], lg[:, t * E:(t + 1) * E], ident)
                mm.then_inc(a_full, 1)

            def gate_up(n):
                g, e, i = n // (E * IC), n // IC % E, n % IC
                k = g * E + e
                if i == 0:
                    pe.wait_ge(ew_in[k % 2], 48 * (k // 2 + 1))
                if n >= 2:
                    pe.wait_ge(hb_rdy, n - 1)
                for w, o in ((eg, 0), (eu, 1)):
                    for c in range(DC):
                        mm = pe.matmul(bank[2 * (n % 2) + o][:, :], w[k % 2][:, c, i * P:(i + 1) * P], xTm[:, c, :],
                                       start=(c == 0), stop=(c == DC - 1))
                mm.then_inc(gu_full, 1)

            def down(n):
                g, e, i = n // (E * IC), n // IC % E, n % IC
                k = g * E + e
                if n % (E * IC) == 0:
                    pe.wait_ge(d_free, jd.n)
                    pe.wait_ge(a_free, ja.n)
                pe.wait_ge(hc_rdy, n + 1)
                for t in range(NT):
                    mm = pe.matmul(bank[4 + t][:, :], hc[n % 2][:, t * P:(t + 1) * P], ed[k % 2][:, i, :],
                                   start=(e == 0 and i == 0), stop=(e == E - 1 and i == IC - 1))
                mm.then_inc(dn_done, 1)

            def moe_step(g, e):
                for i in range(IC):
                    n = (g * E + e) * IC + i
                    if e < E - 1 or i < IC - 1:
                        gate_up(n + 1)
                    down(n)

            pe.wait_ge(par_in, 16)
            pe.wait_ge(sw_in, 32)
            pe.wait_ge(ones_rdy, 1)
            norm_transposes()
            for sg in range(2):
                attn_prep(sg)
                attn_units_start(sg)
                for k in range(NU):
                    attn_unit(sg, k)
                attn_end(sg)
            norm_transposes()
            projections(0)
            norm_transposes()
            for sg in range(2, 4):
                attn_prep(sg)
                attn_units_start(sg)
                for k in range(NU):
                    attn_unit(sg, k)
                attn_end(sg)
            out_proj(0)
            norm_transposes()
            route(0)
            norm_transposes()
            projections(1)
            gate_up(0)
            for e in range(E):
                moe_step(0, e)
            out_proj(1)
            norm_transposes()
            route(1)
            gate_up(E * IC)
            for e in range(E):
                moe_step(1, e)

        @block.scalar
        def _(act):
            ja, chain = Count(), Count()

            def step(ins):
                chain.n += 1
                ins.then_inc(act_step, 1)
                act.wait_ge(act_step, chain.n)

            def job_a():
                ja.n += 1
                act.wait_ge(a_full, ja.n)
                return bank[6 + (ja.n - 1) % 2]

            norms = Count()

            def norm(dst):
                norms.n += 1
                act.wait_ge(var_rdy, norms.n)
                act.activation(rstd[:, :], mv[:, :, 1], ACT.Sqrt, bias=epsc[:, 0:1]).then_inc(std_rdy, 1)
                for c in range(DC):
                    b = job_a()
                    act.activation(dst[:, c, :], b[:, :], ACT.Copy).then_inc(a_free, 1)

            def attn_prep(sg):
                for m in range(DC):
                    b = job_a()
                    o = qT[:, m, :].rearrange("p (b two i) -> p b i two", two=2, i=TI)
                    act.activation(o, b[:, 0:ST].rearrange("p (b i two) -> p b i two", two=2, i=TI), ACT.Identity,
                                   bias=par[:, C_BQ + m:C_BQ + m + 1], scale=DH ** -0.5).then_inc(a_free, 1)
                for c in range(DC):
                    q = QT[:, :, c, :].rearrange("p u (mp k hh i) -> p mp hh k u i", mp=2, k=2, hh=2)
                    for mp in range(DC // 2):
                        for hh in range(2):
                            b = job_a()
                            act.activation(q[:, mp, hh], b[:, :].rearrange("p (k u i) -> p k u i", k=2, u=NU),
                                           ACT.Copy).then_inc(a_free, 1)

            def exps(n):
                act.wait_ge(nm_rdy, n + 1)
                if n >= 2:
                    act.wait_ge(t_full, n - 1)
                for qb in range(QB):
                    ins = act.activation(prob[n % 2][:, qb, :], bank[n % 2][:, qb * KEYS:(qb + 1) * KEYS], ACT.Exp,
                                         bias=nmax[:, n % 2 * QB + qb:n % 2 * QB + qb + 1],
                                         accum_out=rsum[:, n % 2 * QB + qb:n % 2 * QB + qb + 1])
                ins.then_inc(p_exp, 1)

            def copy_probs(n):
                act.wait_ge(t_full, n + 1)
                if n >= 2:
                    act.wait_ge(d_full, ctx_read(n - 2))
                act.activation(probT[n % 2][:, :, :].rearrange("p j q -> p (j q)"), bank[2 + n % 2][:, :], ACT.Copy)\
                   .then_inc(t_copied, 1)

            def attn_end(sg):
                for m in range(DC):
                    b = job_a()
                    o = qT[:, m, :].rearrange("p (b i two) -> p b i two", two=2, i=TI)
                    act.activation(o, b[:, 0:ST].rearrange("p (b two i) -> p b i two", two=2, i=TI), ACT.Identity,
                                   bias=par[:, C_BV + m:C_BV + m + 1]).then_inc(a_free, 1)

            def projections(g):
                b = job_a()
                act.activation(bcT, b[0:2 * NS, :], ACT.Copy).then_inc(a_free, 1)
                act.wait_ge(a_free, ja.n)
                act.nop().then_inc(act_bc, 1)
                if g > 0:
                    act.wait_ge(step_done, steps_per_group * g)
                for k in range(NBK):
                    b = job_a()
                    act.activation(dlt[:, k, :], b[:, :], ACT.Identity, bias=par[:, C_DTB + k:C_DTB + k + 1])\
                       .then_inc(a_free, 1)
                for k in range(NBK):
                    b = job_a()
                    if k >= 2:
                        act.wait_ge(conv_done, g * NBK + k - 1)
                    else:
                        act.wait_ge(pad_rdy, g + 1)
                    act.activation(xi[k % 2][:, :, TAPS - 1:], b[:, :].rearrange("p (b t) -> p b t", b=GB), ACT.Copy)\
                       .then_inc(a_free, 1)
                step(act.activation(acc_[:, :], del_[:, :], ACT.Abs))
                step(act.activation(acc_[:, :], acc_[:, :], ACT.Exp, scale=-1.0))
                act.activation(acc_[:, :], acc_[:, :], ACT.Ln, bias=1.0).then_inc(sp_rdy, 1)
                act.wait_ge(sp_used, g + 1)
                act.activation(acc_[:, :], u_[:, :], ACT.Tanh, scale=0.5).then_inc(tanh_rdy, 1)

            def scan_decay(g, j):
                n = g * steps_per_group + j
                if j == 0:
                    act.wait_ge(dl_rdy, g + 1)
                if n >= 2:
                    act.wait_ge(scan_rd, n - 1)
                s, hf = j // 2, j % 2
                for k in range(HALF):
                    c = C_A + (hf * HALF + k) * NS + s
                    ins = act.activation(dA[n % 2][:, k * GT:(k + 1) * GT], dlt[:, hf * HALF + k, :], ACT.Exp,
                                         scale=par[:, c:c + 1])
                ins.then_inc(da_rdy, 1)

            def route(g):
                b = job_a()
                act.activation(lg, b[:, 0:NT * E], ACT.Exp, scale=-1.0).then_inc(a_free, 1)
                b = job_a()
                act.activation(combT, b[0:E, :], ACT.Copy).then_inc(a_free, 1)
                act.wait_ge(a_free, ja.n)
                act.nop().then_inc(comb_act, 1)

            def gate_tanh(n):
                act.wait_ge(gu_full, n + 1)
                if n >= 2:
                    act.wait_ge(hb_rdy, n - 1)
                act.activation(th[n % 2], bank[2 * (n % 2)][:, :], ACT.Tanh, scale=0.5).then_inc(th_rdy, 1)

            act.wait_ge(par_in, 16)
            act.activation(par[:, C_A:C_A + NBK * NS], par[:, C_A:C_A + NBK * NS], ACT.Exp).then_inc(aexp, 1)
            act.wait_ge(ones_rdy, 1)
            norm(xT)
            for sg in range(2):
                attn_prep(sg)
                for k in range(NU):
                    exps(unit(sg, k))
                    copy_probs(unit(sg, k))
                attn_end(sg)
            norm(xT)
            projections(0)
            norm(xT)
            scan_decay(0, 0)
            scan_decay(0, 1)
            for sg in range(2, 4):
                attn_prep(sg)
                for k in range(NU):
                    n = unit(sg, k)
                    j = 2 * (n - 2 * NU)
                    exps(n)
                    if j + 2 < steps_per_group:
                        scan_decay(0, j + 2)
                    copy_probs(n)
                    if j + 3 < steps_per_group:
                        scan_decay(0, j + 3)
                attn_end(sg)
            norm(xTm)
            route(0)
            norm(xT)
            projections(1)
            scan_decay(1, 0)
            for n in range(E * IC):
                gate_tanh(n)
                if n + 1 < steps_per_group:
                    scan_decay(1, n + 1)
            norm(xTm)
            route(1)
            for n in range(E * IC, 2 * E * IC):
                gate_tanh(n)

        @block.vector
        def _(dve):
            jd, chain = Count(), Count()

            def step(ins):
                chain.n += 1
                ins.then_inc(dve_step, 1)
                dve.wait_ge(dve_step, chain.n)

            def job_d():
                jd.n += 1
                dve.wait_ge(d_full, jd.n)
                return bank[4 + (jd.n - 1) % 2]

            norms = Count()

            def norm(g):
                tiles = [xs[:, g * NT + t, :] for t in range(NT)]
                for t in range(NT):
                    step(dve.bn_stats(st_[:, 6 * t:6 * t + 6], tiles[t]))
                for t in range(NT):
                    ins = dve.bn_aggr(mv[:, t, :], st_[:, 6 * t:6 * t + 6])
                norms.n += 1
                ins.then_inc(var_rdy, 1)
                dve.wait_ge(std_rdy, norms.n)
                step(dve.reciprocal(rstd[:, :], rstd[:, :]))
                for t in range(NT):
                    ins = dve.tensor_scalar(nrm[:, t, :], tiles[t], mv[:, t, 0:1], rstd[:, t:t + 1],
                                            ALU.subtract, ALU.mult)
                ins.then_inc(nrm_rdy, 1)

            def attn_prep(sg):
                b = job_d()
                v = b[0:H, 0:ST].rearrange("p (u i) -> p u i", u=NU).unsqueeze(2).to_broadcast([H, NU, H, TI])
                m = ident[0:H, 0:H].unsqueeze(1).unsqueeze(3).to_broadcast([H, NU, H, TI])
                dve.tensor_tensor(sb8, v, m, ALU.mult).then_inc(d_free, 1)
                dve.wait_ge(d_free, jd.n)
                dve.nop().then_inc(sb8_rdy, 1)

            def neg_max(n):
                dve.wait_ge(s_full, n + 1)
                dve.tensor_reduce(nmax[:, n % 2 * QB:(n % 2 + 1) * QB],
                                  bank[n % 2][:, :].rearrange("p (b k) -> p b k", b=QB), AX_X, ALU.max,
                                  negate=True).then_inc(nm_rdy, 1)

            def normalise(n):
                dve.wait_ge(p_exp, n + 1)
                r = rsum[:, n % 2 * QB:(n % 2 + 1) * QB]
                step(dve.reciprocal(r, r))
                for qb in range(QB):
                    ins = dve.tensor_scalar(prob[n % 2][:, qb, :], prob[n % 2][:, qb, :], r[:, qb:qb + 1], None, ALU.mult)
                ins.then_inc(p_nrm, 1)

            def keep_ctx(k):
                for half in range(2):
                    b = job_d()
                    dve.tensor_copy(QT[:, k, 2 * half:2 * half + 2, :].rearrange("p c q -> p (c q)"), b[:, :])\
                       .then_inc(d_free, 1)

            def attn_end(sg):
                for t in range(ST // P):
                    b = job_d()
                    tile = xs[:, sg * (ST // P) + t, :]
                    dve.tensor_tensor(tile, tile, b[:, :], ALU.add).then_inc(d_free, 1)
                dve.wait_ge(d_free, jd.n)
                dve.nop().then_inc(x1_rdy, ST // P)

            def projections(g):
                for s in range(2):
                    ins = dve.memset(xi[s][:, :, 0:TAPS - 1], 0.0)
                ins.then_inc(pad_rdy, 1)
                for k in range(NBK):
                    dve.wait_ge(a_free, PROJ_JOBS[g] + k + 1)
                    v = u[:, k, :].rearrange("p (b t) -> p b t", b=GB)
                    w = [par[:, C_CW + k * TAPS + q:C_CW + k * TAPS + q + 1] for q in range(TAPS)]
                    src = xi[k % 2]
                    step(dve.tensor_scalar(v, src[:, :, 0:T], w[0], par[:, C_CB + k:C_CB + k + 1], ALU.mult, ALU.add))
                    for q in range(1, TAPS):
                        ins = dve.scalar_tensor_tensor(out=v, in0=src[:, :, q:q + T], scalar=w[q], in1=v,
                                                       op0=ALU.mult, op1=ALU.add)
                        if q < TAPS - 1:
                            step(ins)
                    ins.then_inc(conv_done, 1)
                dve.wait_ge(conv_done, NBK * (g + 1))
                dve.wait_ge(sp_rdy, g + 1)
                dve.scalar_tensor_tensor(out=del_[:, :], in0=del_[:, :], scalar=0.0, in1=acc_[:, :],
                                         op0=ALU.max, op1=ALU.add).then_inc(sp_used, 1)
                dve.wait_ge(sp_used, g + 1)
                dve.wait_ge(tanh_rdy, g + 1)
                step(dve.scalar_tensor_tensor(out=u_[:, :], in0=acc_[:, :], scalar=1.0, in1=u_[:, :],
                                              op0=ALU.add, op1=ALU.mult))
                for k in range(NBK):
                    ins = dve.tensor_scalar(acc[:, k, :], u[:, k, :], par[:, C_D + k:C_D + k + 1], 0.5,
                                            ALU.mult, ALU.mult)
                step(ins)
                step(dve.scalar_tensor_tensor(out=u_[:, :], in0=u_[:, :], scalar=0.5, in1=del_[:, :],
                                              op0=ALU.mult, op1=ALU.mult))
                first = dlt[:, :, :].rearrange("p k (b t) -> p (k b) t", t=T)[:, :, 0:1]
                dve.memset(first, RESET).then_inc(dl_rdy, 1)
                dve.wait_ge(dl_rdy, g + 1)
                dve.nop().then_inc(cv_all, 1)

            def scan_step(g, j):
                n = g * steps_per_group + j
                s, hf = j // 2, j % 2
                k = g * NS + s
                blk = slice(hf * HALF, (hf + 1) * HALF)
                h = hs[n % 2]
                h3 = h.rearrange("p (k t) -> p k t", k=HALF)
                bs, cs = (bcs[s % 2][:, w, :].unsqueeze(1).to_broadcast([P, HALF, GT]) for w in range(2))
                dve.wait_ge(bc_in[s % 2], 16 * (k // 2 + 1))
                step(dve.tensor_tensor(h3, u[:, blk, :], bs, ALU.mult))
                dve.wait_ge(da_rdy, n + 1)
                dve.tensor_tensor_scan(h, dA[n % 2], h, 0.0, ALU.mult, ALU.add).then_inc(scan_rd, 1)
                dve.wait_ge(scan_rd, n + 1)
                step(dve.tensor_tensor(h3, h3, cs, ALU.mult))
                dve.tensor_tensor(acc[:, blk, :], acc[:, blk, :], h3, ALU.add).then_inc(step_done, 1)
                dve.wait_ge(step_done, n + 1)

            def out_proj(g):
                for t in range(NT):
                    b = job_d()
                    tile = xs[:, g * NT + t, :]
                    dve.tensor_tensor(tile, tile, b[:, :], ALU.add).then_inc(d_free, 1)
                dve.wait_ge(d_free, jd.n)

            def route(g, job):
                dve.wait_ge(a_free, job)
                tie4 = par[:, C_T4:C_T4 + NG * NG].rearrange("p (i j) -> p i j", i=NG)
                tie16 = par[:, C_T16:C_T16 + E * E].rearrange("p (i j) -> p i j", i=E)
                eb = par[:, C_EB:C_EB + E].unsqueeze(1).to_broadcast([P, NT, E])

                def rank(out, v, n, tie):
                    gt = rk1[:, 0:NT * n * n].rearrange("p (t i j) -> p t i j", t=NT, i=n)
                    eq = rk2[:, 0:NT * n * n].rearrange("p (t i j) -> p t i j", t=NT, i=n)
                    for t in range(NT):
                        mine = v[:, t, :].unsqueeze(2).to_broadcast([P, n, n])
                        other = v[:, t, :].unsqueeze(1).to_broadcast([P, n, n])
                        dve.tensor_tensor(gt[:, t], other, mine, ALU.is_gt)
                        step(dve.tensor_tensor(eq[:, t], other, mine, ALU.is_equal))
                        step(dve.tensor_tensor(eq[:, t], eq[:, t], tie, ALU.mult))
                        step(dve.tensor_tensor(gt[:, t], gt[:, t], eq[:, t], ALU.add))
                    step(dve.tensor_reduce(out, rk1[:, 0:NT * n * n].rearrange("p (r j) -> p r j", j=n), AX_X, ALU.add))

                step(dve.tensor_scalar(sc, lg, 1.0, None, ALU.add))
                step(dve.reciprocal(sc, sc))
                step(dve.tensor_tensor(sfc.rearrange("p (t e) -> p t e", t=NT),
                                       sc.rearrange("p (t e) -> p t e", t=NT), eb, ALU.add))
                f = sfc.rearrange("p (r k) -> p r k", k=E // NG)
                m = [gs[:, k * NT * NG:(k + 1) * NT * NG] for k in range(4)]
                x0, x1, x2, x3 = (f[:, :, k] for k in range(4))
                dve.tensor_tensor(m[0], x0, x1, ALU.max)
                dve.tensor_tensor(m[1], x2, x3, ALU.max)
                step(dve.tensor_tensor(m[2], x0, x1, ALU.add))
                dve.tensor_tensor(m[3], x2, x3, ALU.add)
                step(dve.tensor_tensor(m[0], m[0], m[1], ALU.add))
                step(dve.tensor_tensor(m[2], m[2], m[3], ALU.max))
                step(dve.tensor_tensor(m[0], m[0], m[2], ALU.max))
                rank(m[1], m[0].rearrange("p (t i) -> p t i", t=NT), NG, tie4)
                step(dve.tensor_scalar(m[1], m[1], 2.0, None, ALU.is_lt))
                step(dve.tensor_tensor(f, f, m[1].unsqueeze(2).to_broadcast([P, NT * NG, E // NG]), ALU.mult))
                rank(lg, sfc.rearrange("p (t e) -> p t e", t=NT), E, tie16)
                step(dve.tensor_scalar(lg, lg, float(TOPK), None, ALU.is_lt))
                step(dve.tensor_tensor(sc, sc, lg, ALU.mult))
                den = gs[:, 0:NT]
                step(dve.tensor_reduce(den, sc.rearrange("p (t e) -> p t e", t=NT), AX_X, ALU.add))
                step(dve.tensor_scalar(den, den, 1e-20, None, ALU.add))
                step(dve.reciprocal(den, den))
                step(dve.tensor_scalar(den, den, 0.5, None, ALU.mult))
                dve.tensor_tensor(lg.rearrange("p (t e) -> p t e", t=NT),
                                  sc.rearrange("p (t e) -> p t e", t=NT),
                                  den.unsqueeze(2).to_broadcast([P, NT, E]), ALU.mult).then_inc(comb_rdy, 1)

            def hidden(n):
                dve.wait_ge(th_rdy, n + 1)
                if n >= 2:
                    dve.wait_ge(hc_rdy, n - 1)
                step(dve.scalar_tensor_tensor(out=hb[n % 2], in0=th[n % 2], scalar=1.0, in1=bank[2 * (n % 2)][:, :],
                                              op0=ALU.add, op1=ALU.mult))
                dve.tensor_tensor(hb[n % 2], hb[n % 2], bank[2 * (n % 2) + 1][:, :], ALU.mult).then_inc(hb_rdy, 1)

            def final(g):
                dve.wait_ge(dn_done, E * IC * (g + 1))
                for t in range(NT):
                    tile = xs[:, g * NT + t, :]
                    dve.tensor_tensor(tile, tile, bank[4 + t][:, :], ALU.add).then_inc(y_read, 1)

            dve.memset(epsc[:, :], EPS)
            dve.memset(ones8[:, :], 1.0).then_inc(ones_rdy, 1)
            dve.wait_ge(par_in, 16)
            step(dve.tensor_scalar(par[:, C_BQ:C_BQ + DC], par[:, C_BQ:C_BQ + DC], DH ** -0.5, None, ALU.mult))
            dve.wait_ge(aexp, 1)
            step(dve.tensor_scalar(par[:, C_A:C_A + NBK * NS], par[:, C_A:C_A + NBK * NS], -1.0, None, ALU.mult))
            dve.wait_ge(x_in, 16)
            norm(0)
            for sg in range(2):
                attn_prep(sg)
                for k in range(NU):
                    neg_max(unit(sg, k))
                    normalise(unit(sg, k))
                    if k >= 1:
                        keep_ctx(k - 1)
                keep_ctx(NU - 1)
                attn_end(sg)
            norm(0)
            projections(0)
            dve.wait_ge(bc_out, 16)
            norm(1)
            for sg in range(2, 4):
                attn_prep(sg)
                for k in range(NU):
                    n = unit(sg, k)
                    j = 2 * (n - 2 * NU)
                    neg_max(n)
                    scan_step(0, j)
                    normalise(n)
                    scan_step(0, j + 1)
                    if k >= 1:
                        keep_ctx(k - 1)
                keep_ctx(NU - 1)
                attn_end(sg)
            out_proj(0)
            norm(0)
            route(0, ROUTE_JOBS[0])
            dve.wait_ge(comb_out, 16)
            norm(1)
            projections(1)
            for n in range(E * IC):
                hidden(n)
                scan_step(1, n)
            final(0)
            dve.wait_ge(bc_out, 32)
            out_proj(1)
            norm(1)
            route(1, ROUTE_JOBS[1])
            for n in range(E * IC, 2 * E * IC):
                hidden(n)
            final(1)

        @block.gpsimd
        def _(pool):
            for n in range(2 * E * IC):
                k = n // IC
                pool.wait_ge(cb_in[k % 2], 16 * (k // 2 + 1))
                pool.wait_ge(hb_rdy, n + 1)
                if n >= 2:
                    pool.wait_ge(dn_done, n - 1)
                pool.tensor_tensor(hc[n % 2], hb[n % 2], cb[k % 2], ALU.mult).then_inc(hc_rdy, 1)


def kernel(**inputs):
    import numpy as np
    import concourse.bacc as bacc
    from concourse.bass_utils import run_bass_kernel_spmd

    a = {k: np.asarray(v) for k, v in inputs.items()}

    def cols(v, n):
        return v.reshape(n, P, -1).transpose(1, 0, 2).reshape(P, -1)

    bk = np.zeros((P, DC, H), np.float32)
    for m in range(DC):
        for hh in range(2):
            bk[hh * DH:(hh + 1) * DH, m, 2 * m + hh] = a["L0_xattn_bk"][m * P + hh * DH:m * P + (hh + 1) * DH]
    tie = [np.broadcast_to(np.tril(np.ones((n, n), np.float32), -1).reshape(1, -1), (P, n * n)) for n in (NG, E)]
    params = np.concatenate([
        cols(a["L0_xattn_bq"], DC), cols(a["L0_xattn_bv"], DC), cols(a["L0_attn_dt_proj_b"], NBK),
        cols(a["L0_attn_conv_w"], NBK), cols(a["L0_attn_conv_b"], NBK), cols(a["L0_attn_D"], NBK),
        cols(a["L0_attn_A_log"], NBK), bk.reshape(P, -1),
        np.broadcast_to(a["L0_ffn_e_bias"].reshape(1, -1), (P, E)), tie[0], tie[1], np.eye(P, dtype=np.float32)], axis=1)
    ctx = a["ctx_1024"]
    data = {
        "x": a["x"].reshape(G * GT, D),
        "ctx_t": ctx.reshape(NB, KEYS, 2, D).transpose(0, 2, 3, 1),
        "ctx_n": ctx,
        "wq_t": a["L0_xattn_Wq"].T, "wk": a["L0_xattn_Wk"], "wv_t": a["L0_xattn_Wv"].T,
        "xp_t": a["L0_attn_x_proj_w"].T, "dt_t": a["L0_attn_dt_proj_w"].T,
        "bc_t": np.concatenate([a["L0_attn_B_proj_w"], a["L0_attn_C_proj_w"]], axis=0).T,
        "ow_t": a["L0_attn_out_proj_w"].T, "gate_t": a["L0_ffn_gate_weight"].T,
        "eg_t": a["L0_ffn_gate_proj"].transpose(0, 2, 1), "eu_t": a["L0_ffn_up_proj"].transpose(0, 2, 1),
        "ed_t": a["L0_ffn_down_proj"].transpose(0, 2, 1),
        "params": params,
    }
    nc = bacc.Bacc("TRN2", target_bir_lowering=False, num_devices=1)
    arrays, args = {}, []
    for name, v in data.items():
        v = np.ascontiguousarray(v)
        arrays[f"in_{name}"] = v
        args.append(nc.dram_tensor(f"in_{name}", v.shape, F32, kind="ExternalInput").ap())
    args.append(nc.dram_tensor("bc_scratch", (G, 2 * NS, GT), F32, kind="Internal").ap())
    args.append(nc.dram_tensor("comb_scratch", (G, E, GT), F32, kind="Internal").ap())
    args.append(nc.dram_tensor("out_0", (G * GT, D), F32, kind="ExternalOutput").ap())
    perceiver_block(nc, *args)
    r = run_bass_kernel_spmd(nc, [arrays], core_ids=[0])
    return r.results[0]["out_0"].reshape(NB, T, D)
```

```python
from contextlib import ExitStack

import concourse.bass as bass
from concourse import mybir

ALU = mybir.AluOpType
ACT = mybir.ActivationFunctionType
F32 = mybir.dt.float32
AX_X = mybir.AxisListType.X

P = 128
D = 512
DC = D // P
T = 64
NB = 16
S_CTX = 512
KEYS = S_CTX // 2
KC = KEYS // P
G = 4
GB = NB // G
GT = GB * T
NT = GT // P
NU = 2 * GB
HALVES = 2
HG = G // HALVES
HT = HG * GT
HNT = HT // P
TI = T // 2
H = 8
DH = D // H
Q = H * TI
QB = Q // P
DI = 1024
NBK = DI // P
NS = 16
SW = NBK * GT
TAPS = 4
E = 16
TOPK = 4
I = 256
IC = I // P
NG = 4
EPS = 1e-5
RESET = 1e30

C_BQ = 0
C_BV = C_BQ + DC
C_DTB = C_BV + DC
C_CW = C_DTB + NBK
C_CB = C_CW + NBK * TAPS
C_D = C_CB + NBK
C_A = C_D + NBK
C_BK = C_A + NBK * NS
C_EB = C_BK + DC * H
C_T4 = C_EB + E
C_T16 = C_T4 + NG * NG
C_ID = C_T16 + E * E
C_END = C_ID + P


def perceiver_block(nc, x, ctx_t, ctx_n, wq_t, wk, wv_t, xp_t, dt_t, bc_t, ow_t, gate_t,
                    eg_t, eu_t, ed_t, params, bc_dram, out):
    with ExitStack() as es:
        def sb(name, cols):
            return es.enter_context(nc.sbuf_tensor(name, [P, cols], F32))

        def sem(name):
            return es.enter_context(nc.semaphore(name))

        xs_ = sb("x_tokens", G * NT * D)
        xs = xs_[:, :].rearrange("p (n d) -> p n d", d=D)
        nrm_ = sb("normed", HNT * D)
        nrm = nrm_[:, :].rearrange("p (n d) -> p n d", d=D)
        sb8 = nrm_[0:H, 0:NU * Q].rearrange("p (u h i) -> p u h i", u=NU, h=H)
        bcT = nrm_[0:2 * NS, 0:GT]
        lg, sc, sfc, gs = (nrm_[:, 1024 + k * HNT * E:1024 + (k + 1) * HNT * E] for k in range(4))
        comb_ = sb("comb", HNT * E)
        xT_ = sb("normed_t", DC * GT)
        xT = xT_[:, :].rearrange("p (c t) -> p c t", c=DC)
        qT_ = sb("q_t", DC * GT)
        qT = qT_[:, :].rearrange("p (m t) -> p m t", m=DC)
        QT_ = sb("queries_ctx", NU * DC * Q)
        QT = QT_[:, :].rearrange("p (u c q) -> p u c q", u=NU, c=DC)
        dtw = QT_[:, 0:4096].rearrange("p (c n) -> p c n", c=DC)
        xp = QT_[:, 4096:8192].rearrange("p (c n) -> p c n", c=DC)
        sp_tmp = QT_[:, 0:SW]
        th_tmp = QT_[:, SW:2 * SW]
        MW = 2 * DC * I + IC * D
        eg = [QT_[:, s * MW:s * MW + 1024].rearrange("p (c i) -> p c i", c=DC) for s in range(2)]
        eu = [QT_[:, s * MW + 1024:s * MW + 2048].rearrange("p (c i) -> p c i", c=DC) for s in range(2)]
        ed = [QT_[:, s * MW + 2048:s * MW + 3072].rearrange("p (c d) -> p c d", c=IC) for s in range(2)]
        ctx_ = sb("ctx", 2 * (DC * KEYS + KC * D))
        ctxT = [ctx_[:, s * 2048:s * 2048 + 1024].rearrange("p (c k) -> p c k", c=DC) for s in range(2)]
        ctxN = [ctx_[:, s * 2048 + 1024:s * 2048 + 2048].rearrange("p (j d) -> p j d", j=KC) for s in range(2)]
        ow_ = sb("out_w", NBK * D)
        ow = ow_[:, :].rearrange("p (k d) -> p k d", k=NBK)
        pp_ = sb("probs", 4 * QB * KEYS)
        prob = [pp_[:, s * 512:(s + 1) * 512].rearrange("p (b k) -> p b k", b=QB) for s in range(2)]
        probT = [pp_[:, 1024 + s * 512:1536 + s * 512].rearrange("p (j q) -> p j q", j=KC) for s in range(2)]
        rk1 = pp_[:, 0:1024]
        rk2 = pp_[:, 1024:2048]
        w_ = sb("attn_weights", 3 * DC * D)
        wq, wkt, wv = (w_[:, k * 2048:(k + 1) * 2048].rearrange("p (c d) -> p c d", c=DC) for k in range(3))
        xTm = w_[:, 0:2048].rearrange("p (c t) -> p c t", c=DC)
        th = [w_[:, 2048 + s * 512:2560 + s * 512] for s in range(2)]
        hc = [w_[:, 3072 + s * 1024:4096 + s * 1024].rearrange("p (i t) -> p i t", i=IC) for s in range(2)]
        dA_ = sb("decay", 2 * SW)
        dA = [dA_[:, s * SW:(s + 1) * SW] for s in range(2)]
        hs_ = sb("state", SW)
        acc_ = sb("y_acc", SW)
        del_ = sb("delta", 2 * SW)
        u_ = sb("u", 2 * SW)
        acc = acc_[:, :].rearrange("p (k t) -> p k t", k=NBK)
        del_s = [del_[:, s * SW:(s + 1) * SW] for s in range(2)]
        u_s = [u_[:, s * SW:(s + 1) * SW] for s in range(2)]
        dlt, u = ([a.rearrange("p (k t) -> p k t", k=NBK) for a in v] for v in (del_s, u_s))
        bcs_ = sb("bc_bcast", 4 * GT)
        bcs = [bcs_[:, s * 2 * GT:(s + 1) * 2 * GT].rearrange("p (w t) -> p w t", w=2) for s in range(2)]
        XP = GB * (T + TAPS - 1)
        xi_ = sb("conv_in", 2 * 2 * XP)
        xi = [xi_[:, s * 2 * XP:(s + 1) * 2 * XP].rearrange("p (k t) -> p k t", t=T + TAPS - 1) for s in range(2)]
        par = sb("params", C_END)
        bcw_ = sb("bc_weights", DC * 2 * NS)
        bcw = bcw_[:, :].rearrange("p (c n) -> p c n", c=DC)
        gwt_ = sb("gate_weights", DC * E)
        gwt = gwt_[:, :].rearrange("p (c n) -> p c n", c=DC)
        ident = par[:, C_ID:C_ID + P]
        st_ = sb("stats", 6 * HNT)
        mv_ = sb("mean_var", 2 * HNT)
        mv = mv_[:, :].rearrange("p (n k) -> p n k", k=2)
        rstd = sb("rstd", HNT)
        nmax = sb("neg_max", 2 * QB)
        rsum = sb("row_sum", 2 * QB)
        ones8 = sb("ones", 1)
        epsc = sb("eps", 1)

        bank = [es.enter_context(nc.psum_tensor(f"bank{i}", [P, 512], F32)) for i in range(8)]

        par_in = sem("params_in")
        x_in = sem("x_in")
        xr_in = sem("x_rest_in")
        sw_in = sem("small_w_in")
        wq_in = sem("wq_in")
        wk_in = sem("wk_in")
        wv_in = sem("wv_in")
        ctxT_in = [sem(f"ctx_t_in{s}") for s in range(2)]
        ctxN_in = [sem(f"ctx_n_in{s}") for s in range(2)]
        dtw_in = sem("dt_w_in")
        xpw_in = sem("xp_w_in")
        ow_in = sem("out_w_in")
        ew_in = [sem(f"expert_w_in{s}") for s in range(2)]
        bc_in = [sem(f"bc_in{s}") for s in range(2)]
        bc_out = sem("bc_written")
        out_done = sem("out_done")
        act_step = sem("act_step")
        dve_step = sem("dve_step")
        aexp = sem("a_exp")
        ones_rdy = sem("constants_ready")
        pad_rdy = sem("conv_pads_ready")
        var_rdy = sem("var_ready")
        std_rdy = sem("std_ready")
        nrm_rdy = sem("norm_ready")
        a_full = sem("bankA_full")
        a_free = sem("bankA_free")
        d_full = sem("bankD_full")
        d_free = sem("bankD_free")
        sb8_rdy = sem("qbk_ready")
        s_full = sem("scores_full")
        nm_rdy = sem("neg_max_ready")
        p_exp = sem("probs_exp")
        sum_rdy = sem("sum_inverted")
        p_nrm = sem("probs_normed")
        t_full = sem("probsT_full")
        t_copied = sem("probsT_copied")
        x1_rdy = sem("attn_added")
        bc_rdy = sem("bc_ready")
        conv_done = sem("conv_done")
        sp_rdy = sem("softplus_ready")
        tanh_rdy = sem("tanh_ready")
        dl_rdy = sem("delta_ready")
        da_rdy = sem("decay_ready")
        scan_rd = sem("decay_read")
        step_done = sem("scan_step_done")
        gu_full = sem("gate_up_full")
        th_rdy = sem("tanh_gate_ready")
        h_rdy = sem("hidden_ready")
        y_full = sem("y_full")
        y_free = sem("y_free")
        out_rdy = sem("out_ready")

        LEAD = 5
        NORM_A = DC * NT // HNT
        ATTN_A = DC + DC * DC + 2 * NU + DC
        PROJ_A = 1 + NBK
        GROUP_A = 2 * NORM_A + ATTN_A + PROJ_A
        CONV_JOBS = [NORM_A + ATTN_A + NORM_A + 1 + g * GROUP_A for g in range(G)]
        last = CONV_JOBS[G - 1] + NBK
        ROUTE_JOBS = [last + (DC + 1) * (h + 1) for h in range(HALVES)]

        class Count:
            n = 0

        def ctx_read(n):
            return NORM_A + n // NU * GROUP_A + DC + DC * DC + 2 * (n % NU + 1)

        block = es.enter_context(nc.Block())

        @block.sync
        def _(sp):
            def load_ctx_t(n):
                if n < G * NU:
                    if n >= 2:
                        sp.wait_ge(s_full, n - 1)
                    sp.dma_start(ctxT[n % 2], ctx_t[n // 2, n % 2].rearrange("(c p) k -> p c k", p=P))\
                      .then_inc(ctxT_in[n % 2], 16)

            def load_ctx_n(n):
                if n < G * NU:
                    if n >= 2:
                        sp.wait_ge(a_full, ctx_read(n - 2))
                    rows = ctx_n[n // 2].rearrange("(j p two) d -> two p j d", p=P, two=2)
                    sp.dma_start(ctxN[n % 2], rows[n % 2]).then_inc(ctxN_in[n % 2], 16)

            def load_proj(g):
                sp.wait_ge(x1_rdy, g + 1)
                sp.dma_start(xp, xp_t.rearrange("(c p) n -> p c n", p=P)).then_inc(xpw_in, 16)
                sp.dma_start(dtw, dt_t.rearrange("(c p) n -> p c n", p=P)).then_inc(dtw_in, 16)

            def store_bc(g):
                sp.wait_ge(bc_rdy, g + 1)
                sp.dma_start(bc_dram[g], bcT).then_inc(bc_out, 16)
                sp.wait_ge(bc_out, 16 * (g + 1))

            def load_bc(k):
                if k >= 2:
                    sp.wait_ge(step_done, k - 1)
                src = bc_dram[k // NS].rearrange("(w s) t -> s w t", w=2)[k % NS]
                sp.dma_start(bcs[k % 2], src.unsqueeze(0).to_broadcast([P, 2, GT])).then_inc(bc_in[k % 2], 16)

            def load_expert(k):
                if k < HALVES * E:
                    e = k % E
                    if k < 2:
                        sp.wait_ge(dl_rdy, G)
                    else:
                        sp.wait_ge(y_full, HNT * (k - 1))
                    sp.dma_start(eg[k % 2], eg_t[e].rearrange("(c p) i -> p c i", p=P)).then_inc(ew_in[k % 2], 16)
                    sp.dma_start(eu[k % 2], eu_t[e].rearrange("(c p) i -> p c i", p=P)).then_inc(ew_in[k % 2], 16)
                    sp.dma_start(ed[k % 2], ed_t[e].rearrange("(c p) d -> p c d", p=P)).then_inc(ew_in[k % 2], 16)

            def store_out(h):
                sp.wait_ge(out_rdy, h + 1)
                sp.dma_start(out[h * HT:(h + 1) * HT].rearrange("(n p) d -> p n d", p=P),
                             xs[:, h * HNT:(h + 1) * HNT, :]).then_inc(out_done, 16)

            sp.dma_start(par[:, :], params).then_inc(par_in, 16)
            x_v = x.rearrange("(n p) d -> p n d", p=P)
            sp.dma_start(xs[:, 0:NT, :], x_v[:, 0:NT, :]).then_inc(x_in, 16)
            sp.dma_start(wq, wq_t.rearrange("(c p) e -> p c e", p=P)).then_inc(wq_in, 16)
            sp.dma_start(wkt, wk.rearrange("(c p) e -> p c e", p=P)).then_inc(wk_in, 16)
            load_ctx_t(0)
            load_ctx_t(1)
            load_ctx_n(0)
            sp.dma_start(wv, wv_t.rearrange("(c p) e -> p c e", p=P)).then_inc(wv_in, 16)
            sp.dma_start(xs[:, NT:, :], x_v[:, NT:, :]).then_inc(xr_in, 16)
            sp.dma_start(bcw, bc_t.rearrange("(c p) e -> p c e", p=P)).then_inc(sw_in, 16)
            sp.dma_start(gwt, gate_t.rearrange("(c p) e -> p c e", p=P)).then_inc(sw_in, 16)
            sp.dma_start(ow, ow_t.rearrange("(k p) d -> p k d", p=P)).then_inc(ow_in, 16)
            for n in range(1, NU + 1):
                load_ctx_t(n + 1)
                load_ctx_n(n)
            load_proj(0)
            store_bc(0)
            load_bc(0)
            load_bc(1)
            for g in range(G - 1):
                for s in range(LEAD):
                    load_bc(g * NS + s + 2)
                for k in range(NU):
                    n = (g + 1) * NU + k + 1
                    load_ctx_t(n + 1)
                    load_ctx_n(n)
                    load_bc(g * NS + LEAD + k + 2)
                load_proj(g + 1)
                for s in range(LEAD + NU + 2, NS):
                    load_bc(g * NS + s)
                store_bc(g + 1)
                load_bc((g + 1) * NS)
                load_bc((g + 1) * NS + 1)
            load_expert(0)
            load_expert(1)
            for e in range(E):
                load_expert(e + 2)
                if e + 2 < NS:
                    load_bc((G - 1) * NS + e + 2)
            store_out(0)
            for e in range(E):
                load_expert(E + e + 2)
            store_out(1)
            sp.wait_ge(out_done, 32)

        @block.tensor
        def _(pe):
            ja, jd, norms = Count(), Count(), Count()

            def job_a():
                if ja.n >= 2:
                    pe.wait_ge(a_free, ja.n - 1)
                ja.n += 1
                return bank[6 + (ja.n - 1) % 2]

            def job_d():
                if jd.n >= 2:
                    pe.wait_ge(d_free, jd.n - 1)
                jd.n += 1
                return bank[4 + (jd.n - 1) % 2]

            def norm_transposes(first, n, new):
                norms.n += new
                pe.wait_ge(nrm_rdy, norms.n)
                for c0 in range(0, DC, HNT // n):
                    b = job_a()
                    for c in range(HNT // n):
                        for t in range(n):
                            mm = pe.transpose(b[:, (c * n + t) * P:(c * n + t + 1) * P],
                                              nrm[:, first + t, (c0 + c) * P:(c0 + c + 1) * P], ident)
                    mm.then_inc(a_full, 1)

            def attn_prep(g):
                if g == 0:
                    pe.wait_ge(wq_in, 16)
                pe.wait_ge(a_free, ja.n)
                for m in range(DC):
                    b = job_a()
                    for c in range(DC):
                        mm = pe.matmul(b[:, 0:GT], wq[:, c, m * P:(m + 1) * P], xT[:, c, :],
                                       start=(c == 0), stop=(c == DC - 1))
                    mm.then_inc(a_full, 1)
                pe.wait_ge(a_free, ja.n)
                b = job_d()
                for m in range(DC):
                    mm = pe.matmul(b[0:H, 0:GT], par[:, C_BK + m * H:C_BK + (m + 1) * H], qT[:, m, :],
                                   start=(m == 0), stop=(m == DC - 1))
                mm.then_inc(d_full, 1)
                if g == 0:
                    pe.wait_ge(wk_in, 16)
                for c in range(DC):
                    for mp in range(DC // 2):
                        pair = [job_a(), job_a()]
                        for k in range(2):
                            m = 2 * mp + k
                            for hh in range(2):
                                r = slice(hh * DH, (hh + 1) * DH)
                                mm = pe.matmul(pair[hh][:, k * GT:(k + 1) * GT], wkt[r, m, c * P:(c + 1) * P],
                                               qT[r, m, :], start=True, stop=True)
                                if k == 1:
                                    mm.then_inc(a_full, 1)
                pe.wait_ge(a_free, ja.n)
                pe.wait_ge(sb8_rdy, g + 1)

            def scores(g, k):
                n = g * NU + k
                pe.wait_ge(ctxT_in[n % 2], 16 * (n // 2 + 1))
                if n >= 2:
                    pe.wait_ge(p_exp, n - 1)
                for qb in range(QB):
                    o = bank[n % 2][:, qb * KEYS:(qb + 1) * KEYS]
                    for c in range(DC):
                        pe.matmul(o, QT[:, k, c, qb * P:(qb + 1) * P], ctxT[n % 2][:, c, :], start=(c == 0), stop=False)
                    mm = pe.matmul(o, sb8[:, k, qb * 4:(qb + 1) * 4, :], ones8[0:H, :].to_broadcast([H, KEYS]),
                                   start=False, stop=True)
                mm.then_inc(s_full, 1)

            def probs_t(g, k):
                n = g * NU + k
                pe.wait_ge(p_nrm, n + 1)
                if n >= 2:
                    pe.wait_ge(t_copied, n - 1)
                for j in range(KC):
                    for qb in range(QB):
                        mm = pe.transpose(bank[2 + n % 2][:, j * Q + qb * P:j * Q + (qb + 1) * P],
                                          prob[n % 2][:, qb, j * P:(j + 1) * P], ident)
                mm.then_inc(t_full, 1)

            def weighted_ctx(g, k):
                n = g * NU + k
                pe.wait_ge(t_copied, n + 1)
                pe.wait_ge(ctxN_in[n % 2], 16 * (n // 2 + 1))
                for half in range(2):
                    b = job_a()
                    for cc in range(2):
                        c = 2 * half + cc
                        for j in range(KC):
                            mm = pe.matmul(b[:, cc * Q:(cc + 1) * Q], ctxN[n % 2][:, j, c * P:(c + 1) * P],
                                           probT[n % 2][:, j, :], start=(j == 0), stop=(j == KC - 1))
                    mm.then_inc(a_full, 1)

            def attention(g):
                attn_prep(g)
                scores(g, 0)
                for k in range(NU):
                    if k + 1 < NU:
                        scores(g, k + 1)
                    if k >= 1:
                        weighted_ctx(g, k - 1)
                    probs_t(g, k)
                weighted_ctx(g, NU - 1)
                if g == 0:
                    pe.wait_ge(wv_in, 16)
                pe.wait_ge(a_free, ja.n)
                for m in range(DC):
                    b = job_a()
                    for hh in range(2):
                        h = 2 * m + hh
                        for c in range(DC):
                            mm = pe.matmul(b[hh * DH:(hh + 1) * DH, 0:GT], wv[:, c, h * DH:(h + 1) * DH],
                                           QT[:, :, c, h * TI:(h + 1) * TI], start=(c == 0), stop=(c == DC - 1))
                    mm.then_inc(a_full, 1)
                pe.wait_ge(a_free, ja.n)
                for t in range(NT):
                    b = job_d()
                    for m in range(DC):
                        mm = pe.transpose(b[:, m * P:(m + 1) * P], qT[:, m, t * P:(t + 1) * P], ident)
                    mm.then_inc(d_full, 1)

            def projections(g):
                if g == 0:
                    pe.wait_ge(sw_in, 32)
                pe.wait_ge(a_free, ja.n)
                b = job_a()
                for c in range(DC):
                    mm = pe.matmul(b[0:2 * NS, 0:GT], bcw[:, c, :], xT[:, c, :], start=(c == 0), stop=(c == DC - 1))
                mm.then_inc(a_full, 1)
                for w, landed in ((xp, xpw_in), (dtw, dtw_in)):
                    pe.wait_ge(landed, 16 * (g + 1))
                    for k in range(0, NBK, 2):
                        b = job_a()
                        for kk in range(2):
                            for c in range(DC):
                                mm = pe.matmul(b[:, kk * GT:(kk + 1) * GT], w[:, c, (k + kk) * P:(k + kk + 1) * P],
                                               xT[:, c, :], start=(c == 0), stop=(c == DC - 1))
                        mm.then_inc(a_full, 1)

            def out_proj(g):
                if g == 0:
                    pe.wait_ge(ow_in, 16)
                if g == G - 1:
                    pe.wait_ge(y_free, HNT * E)
                pe.wait_ge(step_done, NS * (g + 1))
                for t in range(NT):
                    b = job_d()
                    for k in range(NBK):
                        mm = pe.matmul(b[:, :], acc[:, k, t * P:(t + 1) * P], ow[:, k, :],
                                       start=(k == 0), stop=(k == NBK - 1))
                    mm.then_inc(d_full, 1)

            def route():
                norm_transposes(0, HNT, 1)
                pe.wait_ge(a_free, ja.n)
                b = job_a()
                for t in range(HNT):
                    for c in range(DC):
                        mm = pe.matmul(b[:, t * E:(t + 1) * E], xTm[:, c, t * P:(t + 1) * P], gwt[:, c, :],
                                       start=(c == 0), stop=(c == DC - 1))
                mm.then_inc(a_full, 1)

            def gate_up(n):
                k, i = n // IC, n % IC
                if i == 0:
                    pe.wait_ge(ew_in[k % 2], 48 * (k // 2 + 1))
                if n >= 2:
                    pe.wait_ge(h_rdy, n - 1)
                for w, o in ((eg, 0), (eu, 1)):
                    for c in range(DC):
                        mm = pe.matmul(bank[2 * (n % 2) + o][:, :], w[k % 2][:, c, i * P:(i + 1) * P], xTm[:, c, :],
                                       start=(c == 0), stop=(c == DC - 1))
                mm.then_inc(gu_full, 1)

            def down(k):
                pe.wait_ge(h_rdy, IC * (k + 1))
                if k % E > 0:
                    pe.wait_ge(y_free, HNT * k)
                else:
                    pe.wait_ge(d_free, jd.n)
                    pe.wait_ge(a_free, ja.n)
                for t in range(HNT):
                    for i in range(IC):
                        mm = pe.matmul(bank[4 + t][:, :], hc[k % 2][:, i, t * P:(t + 1) * P], ed[k % 2][:, i, :],
                                       start=(i == 0), stop=(i == IC - 1))
                    mm.then_inc(y_full, 1)

            def experts(h):
                gate_up(h * E * IC)
                gate_up(h * E * IC + 1)
                for k in range(h * E, (h + 1) * E):
                    if (k + 1) % E:
                        gate_up(IC * (k + 1))
                    down(k)
                    if (k + 1) % E:
                        gate_up(IC * (k + 1) + 1)

            pe.wait_ge(par_in, 16)
            pe.wait_ge(ones_rdy, 1)
            norm_transposes(0, NT, 1)
            attention(0)
            norm_transposes(0, NT, 2)
            projections(0)
            norm_transposes(NT, NT, 0)
            for g in range(G - 1):
                attention(g + 1)
                norm_transposes(0, NT, 2 if g + 2 < G else 1)
                projections(g + 1)
                if g + 2 < G:
                    norm_transposes(NT, NT, 0)
                out_proj(g)
            route()
            experts(0)
            out_proj(G - 1)
            route()
            experts(1)

        @block.scalar
        def _(act):
            ja, chain, norms = Count(), Count(), Count()

            def step(ins):
                chain.n += 1
                ins.then_inc(act_step, 1)
                act.wait_ge(act_step, chain.n)

            def job_a():
                ja.n += 1
                act.wait_ge(a_full, ja.n)
                return bank[6 + (ja.n - 1) % 2]

            def norm_std(n):
                norms.n += 1
                act.wait_ge(var_rdy, norms.n)
                act.activation(rstd[:, 0:n], mv[:, 0:n, 1], ACT.Sqrt, bias=epsc[:, 0:1]).then_inc(std_rdy, 1)

            def norm_copy(dst, n):
                flat = dst.rearrange("p c t -> p (c t)")
                for c in range(DC * n // HNT):
                    b = job_a()
                    act.activation(flat[:, c * 512:(c + 1) * 512], b[:, :], ACT.Copy).then_inc(a_free, 1)

            def attn_prep(g):
                for m in range(DC):
                    b = job_a()
                    o = qT[:, m, :].rearrange("p (b two i) -> p b i two", two=2, i=TI)
                    act.activation(o, b[:, 0:GT].rearrange("p (b i two) -> p b i two", two=2, i=TI), ACT.Identity,
                                   bias=par[:, C_BQ + m:C_BQ + m + 1], scale=DH ** -0.5).then_inc(a_free, 1)
                lead = list(range(2, LEAD + 2)) if g > 0 else []
                if len(lead) > DC:
                    scan_decay(g - 1, lead.pop(0))
                for c in range(DC):
                    q = QT[:, :, c, :].rearrange("p u (mp k hh i) -> p mp hh k u i", mp=2, k=2, hh=2)
                    for mp in range(DC // 2):
                        for hh in range(2):
                            b = job_a()
                            act.activation(q[:, mp, hh], b[:, :].rearrange("p (k u i) -> p k u i", k=2, u=NU),
                                           ACT.Copy).then_inc(a_free, 1)
                    if lead:
                        scan_decay(g - 1, lead.pop(0))
                assert not lead

            def exps(n):
                act.wait_ge(nm_rdy, n + 1)
                if n >= 2:
                    act.wait_ge(t_full, n - 1)
                for qb in range(QB):
                    ins = act.activation(prob[n % 2][:, qb, :], bank[n % 2][:, qb * KEYS:(qb + 1) * KEYS], ACT.Exp,
                                         bias=nmax[:, n % 2 * QB + qb:n % 2 * QB + qb + 1],
                                         accum_out=rsum[:, n % 2 * QB + qb:n % 2 * QB + qb + 1])
                ins.then_inc(p_exp, 1)

            def normalise(n):
                act.wait_ge(sum_rdy, n + 1)
                for qb in range(QB):
                    ins = act.activation(prob[n % 2][:, qb, :], prob[n % 2][:, qb, :], ACT.Copy,
                                         scale=rsum[:, n % 2 * QB + qb:n % 2 * QB + qb + 1])
                ins.then_inc(p_nrm, 1)

            def keep_ctx(k):
                for half in range(2):
                    b = job_a()
                    act.activation(QT[:, k, 2 * half:2 * half + 2, :].rearrange("p c q -> p (c q)"), b[:, :], ACT.Copy)\
                       .then_inc(a_free, 1)

            def copy_probs(n):
                act.wait_ge(t_full, n + 1)
                if n >= 2:
                    act.wait_ge(a_full, ctx_read(n - 2))
                act.activation(probT[n % 2].rearrange("p j q -> p (j q)"), bank[2 + n % 2][:, :], ACT.Copy)\
                   .then_inc(t_copied, 1)

            def attn_end():
                for m in range(DC):
                    b = job_a()
                    o = qT[:, m, :].rearrange("p (b i two) -> p b i two", two=2, i=TI)
                    act.activation(o, b[:, 0:GT].rearrange("p (b two i) -> p b i two", two=2, i=TI), ACT.Identity,
                                   bias=par[:, C_BV + m:C_BV + m + 1]).then_inc(a_free, 1)

            def proj_bc(g):
                b = job_a()
                act.activation(bcT, b[0:2 * NS, 0:GT], ACT.Copy).then_inc(a_free, 1)
                act.wait_ge(a_free, ja.n)
                act.nop().then_inc(bc_rdy, 1)

            def proj_dt(g, k0):
                b = job_a()
                for k in range(2):
                    ins = act.activation(dlt[g % 2][:, k0 + k, :], b[:, k * GT:(k + 1) * GT], ACT.Identity,
                                         bias=par[:, C_DTB + k0 + k:C_DTB + k0 + k + 1])
                ins.then_inc(a_free, 1)

            def proj_x(g, k0):
                n = g * NBK // 2 + k0 // 2
                b = job_a()
                act.wait_ge(pad_rdy, 1)
                if n >= 2:
                    act.wait_ge(conv_done, n - 1)
                act.activation(xi[n % 2][:, :, TAPS - 1:], b[:, :].rearrange("p (k t) -> p k t", t=T), ACT.Copy)\
                   .then_inc(a_free, 1)

            def softplus(g):
                act.wait_ge(a_free, ja.n)
                step(act.activation(sp_tmp, del_s[g % 2], ACT.Abs))
                step(act.activation(sp_tmp, sp_tmp, ACT.Exp, scale=-1.0))
                act.activation(sp_tmp, sp_tmp, ACT.Ln, bias=1.0).then_inc(sp_rdy, 1)

            def silu(g):
                act.wait_ge(conv_done, (g + 1) * NBK // 2)
                act.activation(th_tmp, u_s[g % 2], ACT.Tanh, scale=0.5).then_inc(tanh_rdy, 1)

            def scan_decay(g, j, first=0, end=NBK):
                n = g * NS + j
                if j == 0 and first == 0:
                    act.wait_ge(dl_rdy, g + 1)
                if n >= 2 and first == 0:
                    act.wait_ge(scan_rd, n - 1)
                for k in range(first, end):
                    c = C_A + k * NS + j
                    ins = act.activation(dA[n % 2][:, k * GT:(k + 1) * GT], dlt[g % 2][:, k, :], ACT.Exp,
                                         scale=par[:, c:c + 1])
                if end == NBK:
                    ins.then_inc(da_rdy, 1)

            def attention_units(g):
                for k in range(NU):
                    n = g * NU + k
                    exps(n)
                    if g > 0:
                        scan_decay(g - 1, LEAD + k + 2, 0, NBK // 2)
                    normalise(n)
                    if k >= 1:
                        keep_ctx(k - 1)
                    if g > 0:
                        scan_decay(g - 1, LEAD + k + 2, NBK // 2)
                    copy_probs(n)
                keep_ctx(NU - 1)

            def gate_tanh(n):
                act.wait_ge(gu_full, n + 1)
                if n >= 2:
                    act.wait_ge(h_rdy, n - 1)
                act.activation(th[n % 2], bank[2 * (n % 2)][:, :], ACT.Tanh, scale=0.5).then_inc(th_rdy, 1)

            def route():
                norm_std(HNT)
                norm_copy(xTm, HNT)
                b = job_a()
                act.activation(lg, b[:, 0:HNT * E], ACT.Exp, scale=-1.0).then_inc(a_free, 1)

            def projections(g):
                late = list(range(LEAD + NU + 2, NS)) if g > 0 else []
                norm_std(NT)
                norm_copy(xT, NT)
                proj_bc(g)
                for k in range(0, NBK, 2):
                    proj_x(g, k)
                    if late:
                        scan_decay(g - 1, late.pop(0))
                assert not late
                for k in range(0, NBK, 2):
                    proj_dt(g, k)
                softplus(g)
                silu(g)
                if g + 1 < G:
                    norm_copy(xT, NT)

            act.wait_ge(par_in, 16)
            act.activation(par[:, C_A:C_A + NBK * NS], par[:, C_A:C_A + NBK * NS], ACT.Exp).then_inc(aexp, 1)
            act.wait_ge(ones_rdy, 1)
            norm_std(NT)
            norm_copy(xT, NT)
            attn_prep(0)
            attention_units(0)
            attn_end()
            norm_std(NT)
            projections(0)
            for g in range(G - 1):
                scan_decay(g, 0)
                scan_decay(g, 1)
                attn_prep(g + 1)
                attention_units(g + 1)
                attn_end()
                if g + 2 < G:
                    norm_std(NT)
                projections(g + 1)
            route()
            scan_decay(G - 1, 0)
            scan_decay(G - 1, 1)
            for n in range(E * IC):
                gate_tanh(n)
                if n % IC == 1 and n // IC + 2 < NS:
                    scan_decay(G - 1, n // IC + 2)
            route()
            for n in range(E * IC, 2 * E * IC):
                gate_tanh(n)

        @block.vector
        def _(dve):
            jd, chain, norms = Count(), Count(), Count()

            def step(ins):
                chain.n += 1
                ins.then_inc(dve_step, 1)
                dve.wait_ge(dve_step, chain.n)

            def job_d():
                jd.n += 1
                dve.wait_ge(d_full, jd.n)
                return bank[4 + (jd.n - 1) % 2]

            def norm(tile0, n, slot):
                tiles = [xs[:, tile0 + t, :] for t in range(n)]
                for t in range(n):
                    step(dve.bn_stats(st_[:, 6 * t:6 * t + 6], tiles[t]))
                for t in range(n):
                    ins = dve.bn_aggr(mv[:, t, :], st_[:, 6 * t:6 * t + 6])
                norms.n += 1
                ins.then_inc(var_rdy, 1)
                dve.wait_ge(std_rdy, norms.n)
                step(dve.reciprocal(rstd[:, 0:n], rstd[:, 0:n]))
                for t in range(n):
                    ins = dve.tensor_scalar(nrm[:, slot + t, :], tiles[t], mv[:, t, 0:1], rstd[:, t:t + 1],
                                            ALU.subtract, ALU.mult)
                ins.then_inc(nrm_rdy, 1)
                dve.wait_ge(nrm_rdy, norms.n)

            def key_bias(g):
                b = job_d()
                dve.wait_ge(bc_out, 16 * g) if g else None
                v = b[0:H, 0:GT].rearrange("p (u i) -> p u i", u=NU).unsqueeze(2).to_broadcast([H, NU, H, TI])
                m = ident[0:H, 0:H].unsqueeze(1).unsqueeze(3).to_broadcast([H, NU, H, TI])
                dve.tensor_tensor(sb8, v, m, ALU.mult).then_inc(d_free, 1)
                dve.wait_ge(d_free, jd.n)
                dve.nop().then_inc(sb8_rdy, 1)

            def neg_max(n):
                dve.wait_ge(s_full, n + 1)
                dve.tensor_reduce(nmax[:, n % 2 * QB:(n % 2 + 1) * QB],
                                  bank[n % 2][:, :].rearrange("p (b k) -> p b k", b=QB), AX_X, ALU.max,
                                  negate=True).then_inc(nm_rdy, 1)

            def add_tiles(g):
                for t in range(NT):
                    b = job_d()
                    tile = xs[:, g * NT + t, :]
                    dve.tensor_tensor(tile, tile, b[:, :], ALU.add).then_inc(d_free, 1)
                dve.wait_ge(d_free, jd.n)

            def conv(g, k0):
                n = g * NBK // 2 + k0 // 2
                dve.wait_ge(a_free, CONV_JOBS[g] + k0 // 2 + 1)
                for q in range(TAPS):
                    for kk in range(2):
                        k = k0 + kk
                        v = u[g % 2][:, k, :].rearrange("p (b t) -> p b t", b=GB)
                        w = par[:, C_CW + k * TAPS + q:C_CW + k * TAPS + q + 1]
                        src = xi[n % 2][:, kk * GB:(kk + 1) * GB, q:q + T]
                        if q == 0:
                            ins = dve.tensor_scalar(v, src, w, par[:, C_CB + k:C_CB + k + 1], ALU.mult, ALU.add)
                        else:
                            ins = dve.scalar_tensor_tensor(out=v, in0=src, scalar=w, in1=v, op0=ALU.mult, op1=ALU.add)
                    if q < TAPS - 1:
                        step(ins)
                ins.then_inc(conv_done, 1)

            def scan_inputs(g):
                d = del_s[g % 2]
                dve.wait_ge(sp_rdy, g + 1)
                step(dve.scalar_tensor_tensor(out=d, in0=d, scalar=0.0, in1=sp_tmp, op0=ALU.max, op1=ALU.add))
                dve.wait_ge(tanh_rdy, g + 1)
                step(dve.scalar_tensor_tensor(out=th_tmp, in0=th_tmp, scalar=1.0, in1=u_s[g % 2],
                                              op0=ALU.add, op1=ALU.mult))
                step(dve.scalar_tensor_tensor(out=u_s[g % 2], in0=th_tmp, scalar=0.5, in1=d,
                                              op0=ALU.mult, op1=ALU.mult))

            def y_start(g):
                for k in range(NBK):
                    ins = dve.tensor_scalar(acc[:, k, :], th_tmp[:, k * GT:(k + 1) * GT], par[:, C_D + k:C_D + k + 1],
                                            0.5, ALU.mult, ALU.mult)
                step(ins)
                first = dlt[g % 2].rearrange("p k (b t) -> p (k b) t", t=T)[:, :, 0:1]
                dve.memset(first, RESET).then_inc(dl_rdy, 1)
                dve.wait_ge(dl_rdy, g + 1)

            def invert_sums(n):
                dve.wait_ge(p_exp, n + 1)
                rs = rsum[:, n % 2 * QB:(n % 2 + 1) * QB]
                dve.reciprocal(rs, rs).then_inc(sum_rdy, 1)

            def scan_step(g, j, unit=None):
                n = g * NS + j
                h = hs_[:, :]
                h3 = h.rearrange("p (k t) -> p k t", k=NBK)
                bs, cs = (bcs[n % 2][:, w, :].unsqueeze(1).to_broadcast([P, NBK, GT]) for w in range(2))
                dve.wait_ge(bc_in[n % 2], 16 * (n // 2 + 1))
                step(dve.tensor_tensor(h3, u[g % 2], bs, ALU.mult))
                if unit is not None:
                    invert_sums(unit)
                dve.wait_ge(da_rdy, n + 1)
                dve.tensor_tensor_scan(h, dA[n % 2], h, 0.0, ALU.mult, ALU.add).then_inc(scan_rd, 1)
                dve.wait_ge(scan_rd, n + 1)
                step(dve.tensor_tensor(h3, h3, cs, ALU.mult))
                dve.tensor_tensor(acc_[:, :], acc_[:, :], h, ALU.add).then_inc(step_done, 1)
                dve.wait_ge(step_done, n + 1)

            def rank(out, v, n, tie):
                gt = rk1[:, 0:HNT * n * n].rearrange("p (t i j) -> p t i j", t=HNT, i=n)
                eq = rk2[:, 0:HNT * n * n].rearrange("p (t i j) -> p t i j", t=HNT, i=n)
                for t in range(HNT):
                    mine = v[:, t, :].unsqueeze(2).to_broadcast([P, n, n])
                    other = v[:, t, :].unsqueeze(1).to_broadcast([P, n, n])
                    dve.tensor_tensor(gt[:, t], other, mine, ALU.is_gt)
                    ins = dve.tensor_tensor(eq[:, t], other, mine, ALU.is_equal)
                step(ins)
                ties = tie.unsqueeze(1).to_broadcast([P, HNT, n * n])
                flat = [r[:, 0:HNT * n * n].rearrange("p (t q) -> p t q", t=HNT) for r in (rk1, rk2)]
                step(dve.tensor_tensor(flat[1], flat[1], ties, ALU.mult))
                step(dve.tensor_tensor(flat[0], flat[0], flat[1], ALU.add))
                step(dve.tensor_reduce(out, rk1[:, 0:HNT * n * n].rearrange("p (r j) -> p r j", j=n), AX_X, ALU.add))

            def route(h):
                if h == 0:
                    dve.wait_ge(bc_out, 16 * G)
                norm(h * HNT, HNT, 0)
                dve.wait_ge(a_free, ROUTE_JOBS[h])
                tie4, tie16 = par[:, C_T4:C_T4 + NG * NG], par[:, C_T16:C_T16 + E * E]
                eb = par[:, C_EB:C_EB + E].unsqueeze(1).to_broadcast([P, HNT, E])
                step(dve.tensor_scalar(sc, lg, 1.0, None, ALU.add))
                step(dve.reciprocal(sc, sc))
                tiles = lambda v: v.rearrange("p (t e) -> p t e", t=HNT)
                step(dve.tensor_tensor(tiles(sfc), tiles(sc), eb, ALU.add))
                f = sfc.rearrange("p (r k) -> p r k", k=E // NG)
                m = [gs[:, k * HNT * NG:(k + 1) * HNT * NG] for k in range(4)]
                x0, x1, x2, x3 = (f[:, :, k] for k in range(4))
                dve.tensor_tensor(m[0], x0, x1, ALU.max)
                dve.tensor_tensor(m[1], x2, x3, ALU.max)
                dve.tensor_tensor(m[2], x0, x1, ALU.add)
                step(dve.tensor_tensor(m[3], x2, x3, ALU.add))
                step(dve.tensor_tensor(m[0], m[0], m[1], ALU.add))
                step(dve.tensor_tensor(m[2], m[2], m[3], ALU.max))
                step(dve.tensor_tensor(m[0], m[0], m[2], ALU.max))
                rank(m[1], tiles(m[0]), NG, tie4)
                step(dve.tensor_scalar(m[1], m[1], 2.0, None, ALU.is_lt))
                step(dve.tensor_tensor(f, f, m[1].unsqueeze(2).to_broadcast([P, HNT * NG, E // NG]), ALU.mult))
                rank(lg, tiles(sfc), E, tie16)
                step(dve.tensor_scalar(lg, lg, float(TOPK), None, ALU.is_lt))
                step(dve.tensor_tensor(sc, sc, lg, ALU.mult))
                den = gs[:, 0:HNT]
                step(dve.tensor_reduce(den, tiles(sc), AX_X, ALU.add))
                step(dve.tensor_scalar(den, den, 1e-20, None, ALU.add))
                step(dve.reciprocal(den, den))
                step(dve.tensor_scalar(den, den, 0.5, None, ALU.mult))
                step(dve.tensor_tensor(tiles(comb_[:, :]), tiles(sc), den.unsqueeze(2).to_broadcast([P, HNT, E]), ALU.mult))

            def hidden(n):
                k, i = n // IC, n % IC
                dve.wait_ge(th_rdy, n + 1)
                if i == 0 and k >= 2:
                    dve.wait_ge(y_full, HNT * (k - 1))
                o = hc[k % 2][:, i, :]
                step(dve.scalar_tensor_tensor(out=o, in0=th[n % 2], scalar=1.0, in1=bank[2 * (n % 2)][:, :],
                                              op0=ALU.add, op1=ALU.mult))
                dve.tensor_tensor(o, o, bank[2 * (n % 2) + 1][:, :], ALU.mult).then_inc(h_rdy, 1)

            def add_expert(k):
                for t in range(HNT):
                    tile = xs[:, (k // E) * HNT + t, :]
                    dve.wait_ge(y_full, HNT * k + t + 1)
                    dve.scalar_tensor_tensor(out=tile, in0=bank[4 + t][:, :], scalar=comb_[:, t * E + k % E:t * E + k % E + 1],
                                             in1=tile, op0=ALU.mult, op1=ALU.add).then_inc(y_free, 1)
                dve.wait_ge(y_free, HNT * (k + 1))

            def experts(h):
                hidden(h * E * IC)
                hidden(h * E * IC + 1)
                for k in range(h * E, (h + 1) * E):
                    if h == 0:
                        scan_step(G - 1, k)
                    if (k + 1) % E:
                        hidden(IC * (k + 1))
                    add_expert(k)
                    if (k + 1) % E:
                        hidden(IC * (k + 1) + 1)
                dve.nop().then_inc(out_rdy, 1)

            dve.memset(epsc[:, :], EPS)
            dve.memset(ones8[:, :], 1.0).then_inc(ones_rdy, 1)
            for s in range(2):
                ins = dve.memset(xi[s][:, :, 0:TAPS - 1], 0.0)
            ins.then_inc(pad_rdy, 1)
            dve.wait_ge(par_in, 16)
            step(dve.tensor_scalar(par[:, C_BQ:C_BQ + DC], par[:, C_BQ:C_BQ + DC], DH ** -0.5, None, ALU.mult))
            dve.wait_ge(aexp, 1)
            step(dve.tensor_scalar(par[:, C_A:C_A + NBK * NS], par[:, C_A:C_A + NBK * NS], -1.0, None, ALU.mult))
            dve.wait_ge(x_in, 16)
            norm(0, NT, 0)
            key_bias(0)
            for k in range(NU):
                neg_max(k)
                invert_sums(k)
            add_tiles(0)
            dve.nop().then_inc(x1_rdy, 1)
            dve.wait_ge(xr_in, 16)
            norm(NT, NT, NT)
            norm(0, NT, 0)
            for k in range(0, NBK, 2):
                conv(0, k)
            scan_inputs(0)
            y_start(0)
            for g in range(G - 1):
                for s in range(LEAD):
                    if s == 1:
                        key_bias(g + 1)
                    scan_step(g, s)
                for k in range(NU):
                    n = (g + 1) * NU + k
                    neg_max(n)
                    scan_step(g, LEAD + k, n)
                scan_step(g, LEAD + NU)
                add_tiles(g + 1)
                dve.nop().then_inc(x1_rdy, 1)
                if g + 2 < G:
                    norm((g + 2) * NT, NT, NT)
                norm((g + 1) * NT, NT, 0)
                for k in range(0, NBK, 2):
                    if LEAD + NU + 1 + k // 2 < NS:
                        scan_step(g, LEAD + NU + 1 + k // 2)
                    conv(g + 1, k)
                scan_inputs(g + 1)
                add_tiles(g)
                y_start(g + 1)
            route(0)
            experts(0)
            add_tiles(G - 1)
            route(1)
            experts(1)


def kernel(**inputs):
    import numpy as np
    import concourse.bacc as bacc
    from concourse.bass_utils import run_bass_kernel_spmd

    a = {k: np.asarray(v) for k, v in inputs.items()}

    def cols(v, n):
        return v.reshape(n, P, -1).transpose(1, 0, 2).reshape(P, -1)

    bk = np.zeros((P, DC, H), np.float32)
    for m in range(DC):
        for hh in range(2):
            bk[hh * DH:(hh + 1) * DH, m, 2 * m + hh] = a["L0_xattn_bk"][m * P + hh * DH:m * P + (hh + 1) * DH]
    tie = [np.broadcast_to(np.tril(np.ones((n, n), np.float32), -1).reshape(1, -1), (P, n * n)) for n in (NG, E)]
    params = np.concatenate([
        cols(a["L0_xattn_bq"], DC), cols(a["L0_xattn_bv"], DC), cols(a["L0_attn_dt_proj_b"], NBK),
        cols(a["L0_attn_conv_w"], NBK), cols(a["L0_attn_conv_b"], NBK), cols(a["L0_attn_D"], NBK),
        cols(a["L0_attn_A_log"], NBK), bk.reshape(P, -1),
        np.broadcast_to(a["L0_ffn_e_bias"].reshape(1, -1), (P, E)), tie[0], tie[1], np.eye(P, dtype=np.float32)], axis=1)
    ctx = a["ctx_1024"]
    data = {
        "x": a["x"].reshape(G * GT, D),
        "ctx_t": ctx.reshape(NB, KEYS, 2, D).transpose(0, 2, 3, 1),
        "ctx_n": ctx,
        "wq_t": a["L0_xattn_Wq"].T, "wk": a["L0_xattn_Wk"], "wv_t": a["L0_xattn_Wv"].T,
        "xp_t": a["L0_attn_x_proj_w"].T, "dt_t": a["L0_attn_dt_proj_w"].T,
        "bc_t": np.concatenate([a["L0_attn_B_proj_w"], a["L0_attn_C_proj_w"]], axis=0).T,
        "ow_t": a["L0_attn_out_proj_w"].T, "gate_t": a["L0_ffn_gate_weight"].T,
        "eg_t": a["L0_ffn_gate_proj"].transpose(0, 2, 1), "eu_t": a["L0_ffn_up_proj"].transpose(0, 2, 1),
        "ed_t": a["L0_ffn_down_proj"].transpose(0, 2, 1),
        "params": params,
    }
    nc = bacc.Bacc("TRN2", target_bir_lowering=False, num_devices=1)
    arrays, args = {}, []
    for name, v in data.items():
        v = np.ascontiguousarray(v)
        arrays[f"in_{name}"] = v
        args.append(nc.dram_tensor(f"in_{name}", v.shape, F32, kind="ExternalInput").ap())
    args.append(nc.dram_tensor("bc_scratch", (G, 2 * NS, GT), F32, kind="Internal").ap())
    args.append(nc.dram_tensor("out_0", (G * GT, D), F32, kind="ExternalOutput").ap())
    perceiver_block(nc, *args)
    r = run_bass_kernel_spmd(nc, [arrays], core_ids=[0])
    return r.results[0]["out_0"].reshape(NB, T, D)
```

```python
from contextlib import ExitStack

import concourse.bass as bass
from concourse import mybir

ALU = mybir.AluOpType
ACT = mybir.ActivationFunctionType
F32 = mybir.dt.float32
F32R = mybir.dt.float32r
AX_X = mybir.AxisListType.X

P = 128
D = 512
DC = D // P
T = 64
NB = 16
S_CTX = 512
KEYS = S_CTX // 2
KC = KEYS // P
G = 4
GB = NB // G
GT = GB * T
NT = GT // P
NU = 2 * GB
TI = T // 2
H = 8
DH = D // H
Q = H * TI
QB = Q // P
DI = 1024
NBK = DI // P
NS = 16
SW = NBK * GT
TAPS = 4
E = 16
TOPK = 4
I = 256
IC = I // P
NG = 4
PIECES = 2
RAW = 5
CA = G - 1
JA = E * CA
JOBS = JA + E
SCAN_FROM = 4
SCAN_JOBS = 39
OUT_JOB = SCAN_FROM + SCAN_JOBS + 1
BK_PER_NORM = 512 // (NT * P)
EPS = 1e-5
RESET = 1e30

C_BQ = 0
C_BV = C_BQ + DC
C_DTB = C_BV + DC
C_CW = C_DTB + NBK
C_CB = C_CW + NBK * TAPS
C_D = C_CB + NBK
C_A = C_D + NBK
C_BK = C_A + NBK * NS
C_EB = C_BK + DC * H
C_T4 = C_EB + E
C_T16 = C_T4 + NG * NG
C_ID = C_T16 + E * E
C_END = C_ID + P


def job(j):
    return (j // CA, j // CA, j % CA) if j < JA else (E + j - JA, j - JA, G - 1)


def first_job(c):
    return c if c < CA else JA


def x_item(j):
    return j + 2 * min(j + 1, CA) + (2 if j >= JA else 0)


def y_item(j):
    return j + (1 if j >= OUT_JOB else 0)


def last_job(k):
    return CA * (k + 1) - 1 if k < E else JA + k - E


def splits(j):
    out = []
    for k in range(1, 2 * E):
        f = CA * k if k < E else JA + k - E
        at = (max(f - 4, -1), f - 3) if k <= E else (f - 2, f - 2)
        out += [(k, p) for p in range(PIECES) if at[p] == j]
    return out


SCAN_PARTS = 4
STATS_UNIT = 3


def scan_parts(j):
    return [(q // SCAN_PARTS, q % SCAN_PARTS) for q in range(SCAN_PARTS, NS * SCAN_PARTS)
            if SCAN_FROM + (q - SCAN_PARTS) * SCAN_JOBS // ((NS - 1) * SCAN_PARTS) == j]


def perceiver_block(nc, x, ctx_t, ctx_n, wq_t, wk, wv_t, xp_t, dt_t, bc_t, ow_t, gate_t,
                    eg_t, eu_t, ed_t, params, bc_dram, out):
    with ExitStack() as es:
        def sb(name, cols, dtype=F32, stack=es):
            return stack.enter_context(nc.sbuf_tensor(name, [P, cols], dtype))

        def sem(name):
            return es.enter_context(nc.semaphore(name))

        xs_ = sb("x_tokens", G * NT * D)
        xs = xs_[:, :].rearrange("p (n d) -> p n d", d=D)
        nrm_ = sb("normed", 2 * NT * D)
        nrm = nrm_[:, :].rearrange("p (n d) -> p n d", d=D)
        sb8 = nrm_[0:H, 0:NU * Q].rearrange("p (u h i) -> p u h i", u=NU, h=H)
        bcT = nrm_[0:2 * NS, 0:GT]
        comb_ = sb("comb", G * NT * E)
        xT_ = sb("normed_t", DC * GT)
        xT = xT_[:, :].rearrange("p (c t) -> p c t", c=DC)
        ow_ = sb("out_w", NBK * D)
        ow = ow_[:, :].rearrange("p (k d) -> p k d", k=NBK)
        dA_ = sb("decay", 2 * SW)
        dA = [dA_[:, s * SW:(s + 1) * SW] for s in range(2)]
        hs_ = sb("state", SW)
        acc_ = sb("y_acc", SW)
        acc = acc_[:, :].rearrange("p (k t) -> p k t", k=NBK)
        del_1 = sb("delta_odd", SW)
        u_1 = sb("u_odd", SW)
        bcs_ = sb("bc_bcast", 4 * GT)
        bcs = [bcs_[:, s * 2 * GT:(s + 1) * 2 * GT].rearrange("p (w t) -> p w t", w=2) for s in range(2)]
        par = sb("params", C_END)
        gwt_ = sb("gate_weights", DC * E)
        gwt = gwt_[:, :].rearrange("p (c n) -> p c n", c=DC)
        ident = par[:, C_ID:C_ID + P]
        lgs = [sb(f"route_logits_{c}", NT * E)[:, :] for c in range(G)]
        sc, sfc, gs = (sb(f"route_{n}", NT * E)[:, :] for n in ("score", "choice", "group"))
        st_ = sb("stats", 6 * G * NT)
        mv_ = sb("mean_var", 2 * NT)
        rstd = sb("rstd", NT)
        mv1_ = sb("mean_var_x", 2 * G * NT)
        rstd1 = sb("rstd_x", G * NT)
        nmax = sb("neg_max", 2 * QB)
        rsum = sb("row_sum", 2 * QB)
        ones8 = sb("ones", 1)
        epsc = sb("eps", 1)

        with ExitStack() as early:
            ctx_ = sb("ctx", 2 * (DC * KEYS + KC * D), stack=early)
            ctxT = [ctx_[:, s * 2048:s * 2048 + 1024].rearrange("p (c k) -> p c k", c=DC) for s in range(2)]
            ctxN = [ctx_[:, s * 2048 + 1024:s * 2048 + 2048].rearrange("p (j d) -> p j d", j=KC) for s in range(2)]
            w_ = sb("attn_weights", 3 * DC * D, stack=early)
            wq, wkt, wv = (w_[:, k * 2048:(k + 1) * 2048].rearrange("p (c d) -> p c d", c=DC) for k in range(3))
            pp_ = sb("probs", 4 * QB * KEYS, stack=early)
            prob = [pp_[:, s * 512:(s + 1) * 512].rearrange("p (b k) -> p b k", b=QB) for s in range(2)]
            probT = [pp_[:, 1024 + s * 512:1536 + s * 512].rearrange("p (j q) -> p j q", j=KC) for s in range(2)]
            qT_ = sb("q_t", DC * GT, stack=early)
            qT = qT_[:, :].rearrange("p (m t) -> p m t", m=DC)
            del_0 = sb("delta_even", SW, stack=early)
            u_0 = sb("u_even", SW, stack=early)
            XP = GB * (T + TAPS - 1)
            xi_ = sb("conv_in", 2 * 2 * XP, stack=early)
            xi = [xi_[:, s * 2 * XP:(s + 1) * 2 * XP].rearrange("p (k t) -> p k t", t=T + TAPS - 1) for s in range(2)]
            bcw_ = sb("bc_weights", DC * 2 * NS, stack=early)
            bcw = bcw_[:, :].rearrange("p (c n) -> p c n", c=DC)
            QT_ = sb("queries_ctx", NU * DC * Q, stack=early)
            QT = QT_[:, :].rearrange("p (u c q) -> p u c q", u=NU, c=DC)
            dtw = QT_[:, 0:4096].rearrange("p (c n) -> p c n", c=DC)
            xp = QT_[:, 4096:8192].rearrange("p (c n) -> p c n", c=DC)
            sp_tmp = QT_[:, 0:SW]
            th_tmp = QT_[:, SW:2 * SW]
        del_s = [del_0[:, :], del_1[:, :]]
        u_s = [u_0[:, :], u_1[:, :]]
        dlt, u = ([a.rearrange("p (k t) -> p k t", k=NBK) for a in v] for v in (del_s, u_s))

        raw = [sb(f"raw_w{q}", 1024)[:, :] for q in range(3)]

        def gate_up_slot(s):
            return [[sb(f"w_{n}{p}_{s}", 1024, F32R)[:, :].rearrange("p (c i) -> p c i", c=DC) for p in range(PIECES)]
                    for n in ("hi", "lo")]

        def input_slot(s):
            return [sb(f"x_{n}_{s}", DC * GT, F32R)[:, :] for n in ("hi", "lo")]

        def down_slot(s):
            return sb(f"w_down_{s}", IC * D)[:, :].rearrange("p (i d) -> p i d", i=IC)

        w_gu = [gate_up_slot(0)]
        xm = [input_slot(0), input_slot(1)]
        hid = [sb(f"hidden_{s}", IC * GT)[:, :] for s in range(2)]
        w_dn = [down_slot(0)]
        w_gu.append(gate_up_slot(1))
        xm.append(input_slot(2))
        w_dn.append(down_slot(1))
        raw += [sb(f"raw_w{q}", 1024)[:, :] for q in range(3, RAW)]
        rank_ = sb("rank_scratch", 2 * NT * E * E)
        rk1, rk2 = (rank_[:, k * NT * E * E:(k + 1) * NT * E * E] for k in range(2))

        bank = [es.enter_context(nc.psum_tensor(f"bank{i}", [P, 512], F32)) for i in range(8)]
        X = [(bank[0], bank[1]), (bank[2], bank[3])]
        Y = [(bank[4], bank[5]), (bank[6], bank[7])]

        par_in = sem("params_in")
        x_in = sem("x_in")
        xr_in = sem("x_rest_in")
        sw_in = sem("small_w_in")
        wq_in = sem("wq_in")
        wk_in = sem("wk_in")
        wv_in = sem("wv_in")
        ctxT_in = [sem(f"ctx_t_in{s}") for s in range(2)]
        ctxN_in = [sem(f"ctx_n_in{s}") for s in range(2)]
        dtw_in = sem("dt_w_in")
        xpw_in = sem("xp_w_in")
        ow_in = sem("out_w_in")
        raw_in = [sem(f"raw_w_in{q}") for q in range(RAW)]
        down_in = [sem(f"down_w_in{s}") for s in range(2)]
        bc_in = [sem(f"bc_in{s}") for s in range(2)]
        bc_out = sem("bc_written")
        out_done = sem("out_done")
        act_step = sem("act_step")
        dve_step = sem("dve_step")
        aexp = sem("a_exp")
        ones_rdy = sem("constants_ready")
        pad_rdy = sem("conv_pads_ready")
        var_rdy = sem("var_ready")
        std_rdy = sem("std_ready")
        nrm_rdy = sem("norm_ready")
        a_full = sem("bankA_full")
        a_free = sem("bankA_free")
        d_full = sem("bankD_full")
        d_free = sem("bankD_free")
        sb8_rdy = sem("qbk_ready")
        q_full = sem("ctx_queries_full")
        q_free = sem("ctx_queries_copied")
        s_full = sem("scores_full")
        nm_rdy = sem("neg_max_ready")
        p_exp = sem("probs_exp")
        sum_rdy = sem("sum_inverted")
        p_nrm = sem("probs_normed")
        t_full = sem("probsT_full")
        t_copied = sem("probsT_copied")
        x1_rdy = sem("attn_added")
        bc_rdy = sem("bc_ready")
        conv_done = sem("conv_done")
        sp_rdy = sem("softplus_ready")
        tanh_rdy = sem("tanh_ready")
        dl_rdy = sem("delta_ready")
        ys_rdy = sem("y_started")
        da_rdy = sem("decay_ready")
        scan_rd = sem("decay_read")
        step_done = sem("scan_step_done")
        w_hi_rdy = sem("w_hi_ready")
        w_rdy = sem("w_split")
        xt_rdy = sem("experts_x_t_ready")
        xm_rdy = sem("experts_x_split")
        lg_rdy = sem("logits_ready")
        x_full = sem("x_pair_full")
        x_free = sem("x_pair_free")
        th_rdy = sem("tanh_gate_ready")
        h_rdy = sem("hidden_ready")
        y_full = sem("y_pair_full")
        y_free = sem("y_pair_free")
        out_rdy = sem("out_ready")

        LEAD, TAIL, PRE = 4, 2, 2
        LN_AFTER = 3
        NORM_A = DC // BK_PER_NORM
        QPAIRS = DC * DC // 2
        ATTN_A = DC + 2 * NU + DC
        PROJ_A = 1 + NBK
        GROUP_A = 2 * NORM_A + ATTN_A + PROJ_A
        CONV_JOBS = [NORM_A + ATTN_A + NORM_A + 1 + NBK // 2 + g * GROUP_A for g in range(G)]

        class Count:
            n = 0

        def ctx_read(n):
            return NORM_A + n // NU * GROUP_A + DC + 2 * (n % NU + 1)

        block = es.enter_context(nc.Block())

        @block.sync
        def _(sp):
            def load_ctx_t(n):
                if n < G * NU:
                    if n >= 2:
                        sp.wait_ge(s_full, n - 1)
                    sp.dma_start(ctxT[n % 2], ctx_t[n // 2, n % 2].rearrange("(c p) k -> p c k", p=P))\
                      .then_inc(ctxT_in[n % 2], 16)

            def load_ctx_n(n):
                if n < G * NU:
                    if n >= 2:
                        sp.wait_ge(a_full, ctx_read(n - 2))
                    rows = ctx_n[n // 2].rearrange("(j p two) d -> two p j d", p=P, two=2)
                    sp.dma_start(ctxN[n % 2], rows[n % 2]).then_inc(ctxN_in[n % 2], 16)

            def load_proj(g):
                sp.wait_ge(x1_rdy, g + 1)
                sp.dma_start(dtw, dt_t.rearrange("(c p) n -> p c n", p=P)).then_inc(dtw_in, 16)
                sp.dma_start(xp, xp_t.rearrange("(c p) n -> p c n", p=P)).then_inc(xpw_in, 16)

            def store_bc(g):
                sp.wait_ge(bc_rdy, g + 1)
                sp.dma_start(bc_dram[g], bcT).then_inc(bc_out, 16)
                sp.wait_ge(bc_out, 16 * (g + 1))

            def load_bc(k):
                if k >= 2:
                    sp.wait_ge(step_done, k - 1)
                src = bc_dram[k // NS].rearrange("(w s) t -> s w t", w=2)[k % NS]
                sp.dma_start(bcs[k % 2], src.unsqueeze(0).to_broadcast([P, 2, GT])).then_inc(bc_in[k % 2], 16)

            def load_raw(q):
                if q < 2 * E * PIECES:
                    if q >= RAW:
                        sp.wait_ge(w_rdy, q - RAW + 1)
                    elif q == 0:
                        sp.wait_ge(x1_rdy, G)
                    elif q == 3:
                        sp.wait_ge(ys_rdy, G)
                    w = (eg_t, eu_t)[q % 2][q // 2 % E]
                    sp.dma_start(raw[q % RAW].rearrange("p (c i) -> p c i", c=DC),
                                 w.rearrange("(c p) i -> p c i", p=P)).then_inc(raw_in[q % RAW], 16)

            def load_down(k):
                if k < 2 * E:
                    if k == 1:
                        sp.wait_ge(ys_rdy, G)
                    elif k >= 2:
                        sp.wait_ge(y_full, y_item(last_job(k - 2)) + 1)
                    sp.dma_start(w_dn[k % 2], ed_t[k % E].rearrange("(c p) d -> p c d", p=P)).then_inc(down_in[k % 2], 16)

            def store_out(first, end, ready):
                sp.wait_ge(out_rdy, ready)
                sp.dma_start(out[first * P:end * P].rearrange("(n p) d -> p n d", p=P), xs[:, first:end, :])\
                  .then_inc(out_done, 16)

            sp.dma_start(par[:, :], params).then_inc(par_in, 16)
            x_v = x.rearrange("(n p) d -> p n d", p=P)
            sp.dma_start(xs[:, 0:NT, :], x_v[:, 0:NT, :]).then_inc(x_in, 16)
            sp.dma_start(wq, wq_t.rearrange("(c p) e -> p c e", p=P)).then_inc(wq_in, 16)
            sp.dma_start(wkt, wk.rearrange("(c p) e -> p c e", p=P)).then_inc(wk_in, 16)
            load_ctx_t(0)
            load_ctx_t(1)
            load_ctx_n(0)
            sp.dma_start(wv, wv_t.rearrange("(c p) e -> p c e", p=P)).then_inc(wv_in, 16)
            sp.dma_start(xs[:, NT:, :], x_v[:, NT:, :]).then_inc(xr_in, 16)
            sp.dma_start(bcw, bc_t.rearrange("(c p) e -> p c e", p=P)).then_inc(sw_in, 16)
            sp.dma_start(gwt, gate_t.rearrange("(c p) e -> p c e", p=P)).then_inc(sw_in, 16)
            sp.dma_start(ow, ow_t.rearrange("(k p) d -> p k d", p=P)).then_inc(ow_in, 16)
            for n in range(1, NU + 1):
                load_ctx_t(n + 1)
                load_ctx_n(n)
            load_proj(0)
            store_bc(0)
            load_bc(0)
            load_bc(1)
            for g in range(G - 1):
                for s in range(LEAD):
                    load_bc(g * NS + s + 2)
                for k in range(NU):
                    n = (g + 1) * NU + k + 1
                    load_ctx_t(n + 1)
                    load_ctx_n(n)
                    load_bc(g * NS + LEAD + k + 2)
                for s in range(LEAD + NU + 2, min(NS, LEAD + NU + TAIL + 2)):
                    load_bc(g * NS + s)
                load_proj(g + 1)
                for s in range(LEAD + NU + TAIL + 2, NS):
                    load_bc(g * NS + s)
                if g + 1 == G - 1:
                    load_raw(0)
                    load_raw(1)
                    load_raw(2)
                    load_down(0)
                store_bc(g + 1)
                load_bc((g + 1) * NS)
                load_bc((g + 1) * NS + 1)
            for q in range(3, RAW + PIECES):
                load_raw(q)
            load_down(1)
            load_bc((G - 1) * NS + 2)
            for j in range(-1, JOBS):
                for k, p in splits(j):
                    load_raw(k * PIECES + p + RAW)
                if j >= 1 and last_job(job(j - 1)[0]) == j - 1:
                    load_down(job(j - 1)[0] + 2)
                for state, part in scan_parts(j):
                    if part == SCAN_PARTS - 1 and state + 2 < NS:
                        load_bc((G - 1) * NS + state + 2)
            store_out(0, CA * NT, 1)
            store_out(CA * NT, G * NT, 2)
            sp.wait_ge(out_done, 32)

        @block.tensor
        def _(pe):
            ja, jd, norms = Count(), Count(), Count()

            def job_a():
                if ja.n >= 2:
                    pe.wait_ge(a_free, ja.n - 1)
                ja.n += 1
                return bank[6 + (ja.n - 1) % 2]

            def job_d():
                if jd.n >= 2:
                    pe.wait_ge(d_free, jd.n - 1)
                jd.n += 1
                return bank[4 + (jd.n - 1) % 2]

            def norm_transposes(first, n):
                norms.n += 1
                pe.wait_ge(nrm_rdy, norms.n)
                for c0 in range(0, DC, BK_PER_NORM):
                    b = job_a()
                    for c in range(BK_PER_NORM):
                        for t in range(n):
                            mm = pe.transpose(b[:, (c * n + t) * P:(c * n + t + 1) * P],
                                              nrm[:, first + t, (c0 + c) * P:(c0 + c + 1) * P], ident)
                    mm.then_inc(a_full, 1)

            def attn_prep(g):
                if g == 0:
                    pe.wait_ge(wq_in, 16)
                pe.wait_ge(a_free, ja.n)
                for m in range(DC):
                    b = job_a()
                    for c in range(DC):
                        mm = pe.matmul(b[:, 0:GT], wq[:, c, m * P:(m + 1) * P], xT[:, c, :],
                                       start=(c == 0), stop=(c == DC - 1))
                    mm.then_inc(a_full, 1)
                pe.wait_ge(a_free, ja.n)
                b = job_d()
                for m in range(DC):
                    mm = pe.matmul(b[0:H, 0:GT], par[:, C_BK + m * H:C_BK + (m + 1) * H], qT[:, m, :],
                                   start=(m == 0), stop=(m == DC - 1))
                mm.then_inc(d_full, 1)
                if g == 0:
                    pe.wait_ge(wk_in, 16)
                for c in range(DC):
                    for mp in range(DC // 2):
                        n = g * QPAIRS + c * DC // 2 + mp
                        if n >= 2:
                            pe.wait_ge(q_free, n - 1)
                        pair = X[n % 2]
                        for k in range(2):
                            m = 2 * mp + k
                            for hh in range(2):
                                r = slice(hh * DH, (hh + 1) * DH)
                                mm = pe.matmul(pair[hh][:, k * GT:(k + 1) * GT], wkt[r, m, c * P:(c + 1) * P],
                                               qT[r, m, :], start=True, stop=True)
                        mm.then_inc(q_full, 1)
                pe.wait_ge(q_free, (g + 1) * QPAIRS)
                pe.wait_ge(sb8_rdy, g + 1)

            def scores(g, k):
                n = g * NU + k
                pe.wait_ge(ctxT_in[n % 2], 16 * (n // 2 + 1))
                if n >= 2:
                    pe.wait_ge(p_exp, n - 1)
                for qb in range(QB):
                    o = bank[n % 2][:, qb * KEYS:(qb + 1) * KEYS]
                    for c in range(DC):
                        pe.matmul(o, QT[:, k, c, qb * P:(qb + 1) * P], ctxT[n % 2][:, c, :], start=(c == 0), stop=False)
                    mm = pe.matmul(o, sb8[:, k, qb * 4:(qb + 1) * 4, :], ones8[0:H, :].to_broadcast([H, KEYS]),
                                   start=False, stop=True)
                mm.then_inc(s_full, 1)

            def probs_t(g, k):
                n = g * NU + k
                pe.wait_ge(p_nrm, n + 1)
                if n >= 2:
                    pe.wait_ge(t_copied, n - 1)
                for j in range(KC):
                    for qb in range(QB):
                        mm = pe.transpose(bank[2 + n % 2][:, j * Q + qb * P:j * Q + (qb + 1) * P],
                                          prob[n % 2][:, qb, j * P:(j + 1) * P], ident)
                mm.then_inc(t_full, 1)

            def weighted_ctx(g, k):
                n = g * NU + k
                pe.wait_ge(t_copied, n + 1)
                pe.wait_ge(ctxN_in[n % 2], 16 * (n // 2 + 1))
                for half in range(2):
                    b = job_a()
                    for cc in range(2):
                        c = 2 * half + cc
                        for j in range(KC):
                            mm = pe.matmul(b[:, cc * Q:(cc + 1) * Q], ctxN[n % 2][:, j, c * P:(c + 1) * P],
                                           probT[n % 2][:, j, :], start=(j == 0), stop=(j == KC - 1))
                    mm.then_inc(a_full, 1)

            def attention(g):
                attn_prep(g)
                scores(g, 0)
                for k in range(NU):
                    if k + 1 < NU:
                        scores(g, k + 1)
                    if k >= 1:
                        weighted_ctx(g, k - 1)
                    probs_t(g, k)
                weighted_ctx(g, NU - 1)
                if g == 0:
                    pe.wait_ge(wv_in, 16)
                pe.wait_ge(a_free, ja.n)
                for m in range(DC):
                    b = job_a()
                    for hh in range(2):
                        h = 2 * m + hh
                        for c in range(DC):
                            mm = pe.matmul(b[hh * DH:(hh + 1) * DH, 0:GT], wv[:, c, h * DH:(h + 1) * DH],
                                           QT[:, :, c, h * TI:(h + 1) * TI], start=(c == 0), stop=(c == DC - 1))
                    mm.then_inc(a_full, 1)
                pe.wait_ge(a_free, ja.n)
                for t in range(NT):
                    b = job_d()
                    for m in range(DC):
                        mm = pe.transpose(b[:, m * P:(m + 1) * P], qT[:, m, t * P:(t + 1) * P], ident)
                    mm.then_inc(d_full, 1)

            def projections(g):
                if g == 0:
                    pe.wait_ge(sw_in, 32)
                pe.wait_ge(a_free, ja.n)
                b = job_a()
                for c in range(DC):
                    mm = pe.matmul(b[0:2 * NS, 0:GT], bcw[:, c, :], xT[:, c, :], start=(c == 0), stop=(c == DC - 1))
                mm.then_inc(a_full, 1)
                for w, landed in ((dtw, dtw_in), (xp, xpw_in)):
                    pe.wait_ge(landed, 16 * (g + 1))
                    for k in range(0, NBK, 2):
                        b = job_a()
                        for kk in range(2):
                            for c in range(DC):
                                mm = pe.matmul(b[:, kk * GT:(kk + 1) * GT], w[:, c, (k + kk) * P:(k + kk + 1) * P],
                                               xT[:, c, :], start=(c == 0), stop=(c == DC - 1))
                        mm.then_inc(a_full, 1)

            def out_proj(g):
                if g == 0:
                    pe.wait_ge(ow_in, 16)
                pe.wait_ge(step_done, NS * (g + 1))
                for t in range(NT):
                    b = job_d()
                    for k in range(NBK):
                        mm = pe.matmul(b[:, :], acc[:, k, t * P:(t + 1) * P], ow[:, k, :],
                                       start=(k == 0), stop=(k == NBK - 1))
                    mm.then_inc(d_full, 1)

            def x_pair(n):
                if n >= 2:
                    pe.wait_ge(x_free, n - 1)
                return X[n % 2]

            def prepare(c):
                n = x_item(first_job(c)) - 2
                b = x_pair(n)
                norms.n += 1
                pe.wait_ge(nrm_rdy, norms.n)
                for k in range(DC):
                    for t in range(NT):
                        o = (k % BK_PER_NORM * NT + t) * P
                        mm = pe.transpose(b[k // BK_PER_NORM][:, o:o + P], nrm[:, (c + 1) % 2 * NT + t, k * P:(k + 1) * P], ident)
                mm.then_inc(x_full, 1)
                b = x_pair(n + 1)
                pe.wait_ge(xt_rdy, c + 1)
                for t in range(NT):
                    for k in range(DC):
                        mm = pe.matmul(b[0][:, t * E:(t + 1) * E], xT[:, k, t * P:(t + 1) * P], gwt[:, k, :],
                                       start=(k == 0), stop=(k == DC - 1))
                mm.then_inc(x_full, 1)

            def split_matmul(o, w, x, chunks):
                terms = [(a, b, k) for a, b in ((0, 0), (0, 1), (1, 0)) for k in range(chunks)]
                for q, (a, b, k) in enumerate(terms):
                    mm = pe.matmul(o, w[a](k), x[b](k), start=(q == 0), stop=(q == len(terms) - 1))
                return mm

            def gate_up(j):
                k, e, c = job(j)
                b = x_pair(x_item(j))
                if first_job(c) == j:
                    pe.wait_ge(xm_rdy, c + 1)
                x_parts = [(lambda q, v=v: v[:, q * GT:(q + 1) * GT]) for v in xm[c % CA]]
                for p in range(PIECES):
                    pe.wait_ge(w_rdy, k * PIECES + p + 1)
                    for i in range(IC):
                        w_parts = [(lambda q, v=v: v[p][:, q, i * P:(i + 1) * P]) for v in w_gu[k % 2]]
                        mm = split_matmul(b[p][:, i * GT:(i + 1) * GT], w_parts, x_parts, DC)
                mm.then_inc(x_full, 1)

            def y_pair(n):
                if n >= 2:
                    pe.wait_ge(y_free, n - 1)
                return Y[n % 2]

            def down(j):
                k, e, c = job(j)
                b = y_pair(y_item(j))
                if j == 0:
                    pe.wait_ge(d_free, jd.n)
                    pe.wait_ge(a_free, ja.n)
                pe.wait_ge(down_in[k % 2], 16 * (k // 2 + 1))
                pe.wait_ge(h_rdy, j + 1)
                for t in range(NT):
                    for i in range(IC):
                        mm = pe.matmul(b[t][:, :], hid[j % 2][:, i * GT + t * P:i * GT + (t + 1) * P],
                                       w_dn[k % 2][:, i, :], start=(i == 0), stop=(i == IC - 1))
                mm.then_inc(y_full, 1)

            def last_out_proj():
                b = y_pair(y_item(OUT_JOB) - 1)
                pe.wait_ge(step_done, NS * G)
                for t in range(NT):
                    for k in range(NBK):
                        mm = pe.matmul(b[t][:, :], acc[:, k, t * P:(t + 1) * P], ow[:, k, :],
                                       start=(k == 0), stop=(k == NBK - 1))
                mm.then_inc(y_full, 1)

            pe.wait_ge(par_in, 16)
            pe.wait_ge(ones_rdy, 1)
            norm_transposes(0, NT)
            attention(0)
            norm_transposes(0, NT)
            projections(0)
            norm_transposes(NT, NT)
            for g in range(G - 1):
                attention(g + 1)
                norm_transposes(0, NT)
                projections(g + 1)
                if g + 2 < G:
                    norm_transposes(NT, NT)
                else:
                    prepare(0)
                out_proj(g)
            for j in range(-2, JOBS):
                if j + 2 < JOBS:
                    if j + 2 > 0 and first_job(job(j + 2)[2]) == j + 2:
                        prepare(job(j + 2)[2])
                    gate_up(j + 2)
                if j == OUT_JOB:
                    last_out_proj()
                if j >= 0:
                    down(j)

        @block.scalar
        def _(act):
            ja, chain, norms = Count(), Count(), Count()

            def step(ins):
                chain.n += 1
                ins.then_inc(act_step, 1)
                act.wait_ge(act_step, chain.n)

            def job_a():
                ja.n += 1
                act.wait_ge(a_full, ja.n)
                return bank[6 + (ja.n - 1) % 2]

            def norm_std(n, var=mv_, std=rstd, first=0):
                norms.n += 1
                act.wait_ge(var_rdy, norms.n)
                v = var[:, :].rearrange("p (n k) -> p n k", k=2)
                act.activation(std[:, first:first + n], v[:, first:first + n, 1], ACT.Sqrt, bias=epsc[:, 0:1])\
                   .then_inc(std_rdy, 1)

            def norm_copy(dst, n):
                flat = dst.rearrange("p c t -> p (c t)")
                for c in range(DC // BK_PER_NORM):
                    b = job_a()
                    act.activation(flat[:, c * 512:(c + 1) * 512], b[:, :], ACT.Copy).then_inc(a_free, 1)

            def attn_prep(g):
                for m in range(DC):
                    b = job_a()
                    o = qT[:, m, :].rearrange("p (b two i) -> p b i two", two=2, i=TI)
                    act.activation(o, b[:, 0:GT].rearrange("p (b i two) -> p b i two", two=2, i=TI), ACT.Identity,
                                   bias=par[:, C_BQ + m:C_BQ + m + 1], scale=DH ** -0.5).then_inc(a_free, 1)
                lead = list(range(2, LEAD + 2)) if g > 0 else []
                if len(lead) > DC:
                    scan_decay(g - 1, lead.pop(0))
                for c in range(DC):
                    q = QT[:, :, c, :].rearrange("p u (mp k hh i) -> p mp hh k u i", mp=2, k=2, hh=2)
                    for mp in range(DC // 2):
                        n = g * QPAIRS + c * DC // 2 + mp
                        act.wait_ge(q_full, n + 1)
                        for hh in range(2):
                            ins = act.activation(q[:, mp, hh], X[n % 2][hh][:, :].rearrange("p (k u i) -> p k u i", k=2, u=NU),
                                                 ACT.Copy)
                        ins.then_inc(q_free, 1)
                    if lead:
                        scan_decay(g - 1, lead.pop(0))
                assert not lead

            def exps(n):
                act.wait_ge(nm_rdy, n + 1)
                if n >= 2:
                    act.wait_ge(t_full, n - 1)
                for qb in range(QB):
                    ins = act.activation(prob[n % 2][:, qb, :], bank[n % 2][:, qb * KEYS:(qb + 1) * KEYS], ACT.Exp,
                                         bias=nmax[:, n % 2 * QB + qb:n % 2 * QB + qb + 1],
                                         accum_out=rsum[:, n % 2 * QB + qb:n % 2 * QB + qb + 1])
                ins.then_inc(p_exp, 1)

            def normalise(n):
                act.wait_ge(sum_rdy, n + 1)
                for qb in range(QB):
                    ins = act.activation(prob[n % 2][:, qb, :], prob[n % 2][:, qb, :], ACT.Copy,
                                         scale=rsum[:, n % 2 * QB + qb:n % 2 * QB + qb + 1])
                ins.then_inc(p_nrm, 1)

            def keep_ctx(k):
                for half in range(2):
                    b = job_a()
                    act.activation(QT[:, k, 2 * half:2 * half + 2, :].rearrange("p c q -> p (c q)"), b[:, :], ACT.Copy)\
                       .then_inc(a_free, 1)

            def copy_probs(n):
                act.wait_ge(t_full, n + 1)
                if n >= 2:
                    act.wait_ge(a_full, ctx_read(n - 2))
                act.activation(probT[n % 2].rearrange("p j q -> p (j q)"), bank[2 + n % 2][:, :], ACT.Copy)\
                   .then_inc(t_copied, 1)

            def attn_end():
                for m in range(DC):
                    b = job_a()
                    o = qT[:, m, :].rearrange("p (b i two) -> p b i two", two=2, i=TI)
                    act.activation(o, b[:, 0:GT].rearrange("p (b two i) -> p b i two", two=2, i=TI), ACT.Identity,
                                   bias=par[:, C_BV + m:C_BV + m + 1]).then_inc(a_free, 1)

            def proj_bc(g):
                b = job_a()
                act.activation(bcT, b[0:2 * NS, 0:GT], ACT.Copy).then_inc(a_free, 1)
                act.wait_ge(a_free, ja.n)
                act.nop().then_inc(bc_rdy, 1)

            def proj_dt(g, k0):
                b = job_a()
                for k in range(2):
                    ins = act.activation(dlt[g % 2][:, k0 + k, :], b[:, k * GT:(k + 1) * GT], ACT.Identity,
                                         bias=par[:, C_DTB + k0 + k:C_DTB + k0 + k + 1])
                ins.then_inc(a_free, 1)

            def proj_x(g, k0):
                n = g * NBK // 2 + k0 // 2
                b = job_a()
                act.wait_ge(pad_rdy, 1)
                if n >= 2:
                    act.wait_ge(conv_done, n - 1)
                act.activation(xi[n % 2][:, :, TAPS - 1:], b[:, :].rearrange("p (k t) -> p k t", t=T), ACT.Copy)
                for kk in range(2):
                    k = k0 + kk
                    w = C_CW + k * TAPS + TAPS - 1
                    ins = act.activation(u[g % 2][:, k, :], b[:, kk * GT:(kk + 1) * GT], ACT.Identity,
                                         bias=par[:, C_CB + k:C_CB + k + 1], scale=par[:, w:w + 1])
                ins.then_inc(a_free, 1)

            def softplus_exp(g):
                act.wait_ge(a_free, CONV_JOBS[g])
                step(act.activation(sp_tmp, del_s[g % 2], ACT.Abs))
                act.activation(sp_tmp, sp_tmp, ACT.Exp, scale=-1.0).then_inc(act_step, 1)
                chain.n += 1

            def softplus_ln(g):
                act.wait_ge(act_step, chain.n)
                act.activation(sp_tmp, sp_tmp, ACT.Ln, bias=1.0).then_inc(sp_rdy, 1)

            def silu(g):
                act.wait_ge(conv_done, (g + 1) * NBK // 2)
                act.activation(th_tmp, u_s[g % 2], ACT.Tanh, scale=0.5).then_inc(tanh_rdy, 1)

            def y_start(g):
                act.wait_ge(dl_rdy, g + 1)
                if g > 0:
                    act.wait_ge(d_full, (g + 1) * (1 + NT) + g * NT)
                for k in range(NBK):
                    ins = act.activation(acc[:, k, :], th_tmp[:, k * GT:(k + 1) * GT], ACT.Copy,
                                         scale=par[:, C_D + k:C_D + k + 1])
                ins.then_inc(ys_rdy, 1)
                act.wait_ge(ys_rdy, g + 1)

            def scan_decay(g, j, first=0, end=NBK):
                n = g * NS + j
                if j == 0 and first == 0:
                    act.wait_ge(dl_rdy, g + 1)
                if n >= 2 and first == 0:
                    act.wait_ge(scan_rd, n - 1)
                for k in range(first, end):
                    c = C_A + k * NS + j
                    ins = act.activation(dA[n % 2][:, k * GT:(k + 1) * GT], dlt[g % 2][:, k, :], ACT.Exp,
                                         scale=par[:, c:c + 1])
                if end == NBK:
                    ins.then_inc(da_rdy, 1)

            def attention_units(g):
                for k in range(NU):
                    n = g * NU + k
                    if n == STATS_UNIT:
                        norm_std((G - 1) * NT, mv1_, rstd1, NT)
                    exps(n)
                    if g > 0:
                        scan_decay(g - 1, LEAD + k + 2, 0, NBK // 2)
                    normalise(n)
                    if k >= 1:
                        keep_ctx(k - 1)
                    if g > 0:
                        scan_decay(g - 1, LEAD + k + 2, NBK // 2)
                    copy_probs(n)
                keep_ctx(NU - 1)

            def split_hi(k, p):
                q = k * PIECES + p
                act.wait_ge(raw_in[q % RAW], 16 * (q // RAW + 1))
                if k >= 2:
                    act.wait_ge(x_full, x_item(last_job(k - 2)) + 1)
                act.activation(w_gu[k % 2][0][p].rearrange("p c i -> p (c i)"), raw[q % RAW], ACT.Copy).then_inc(w_hi_rdy, 1)

            def prepare(c):
                n = x_item(first_job(c)) - 2
                act.wait_ge(x_full, n + 1)
                for k in range(2):
                    ins = act.activation(xT_[:, k * 512:(k + 1) * 512], X[n % 2][k][:, :], ACT.Copy)
                    ins = act.activation(xm[c % CA][0][:, k * 512:(k + 1) * 512], X[n % 2][k][:, :], ACT.Copy)
                ins.then_inc(xt_rdy, 1)
                if c + 1 < CA:
                    norm_std(NT)
                act.wait_ge(x_full, n + 2)
                act.activation(lgs[c], X[(n + 1) % 2][0][:, 0:NT * E], ACT.Exp, scale=-1.0).then_inc(lg_rdy, 1)

            def gate_tanh(j):
                n = x_item(j)
                act.wait_ge(x_full, n + 1)
                if j >= 2:
                    act.wait_ge(y_full, y_item(j - 2) + 1)
                act.activation(hid[j % 2], X[n % 2][0][:, :], ACT.Tanh, scale=0.5).then_inc(th_rdy, 1)

            def projections(g):
                late = list(range(LEAD + NU + TAIL + 1, NS)) if g > 0 else []
                norm_std(NT)
                if g + 1 == G:
                    norm_std(NT)
                norm_copy(xT, NT)
                proj_bc(g)
                for k in range(0, NBK, 2):
                    proj_dt(g, k)
                    if late:
                        scan_decay(g - 1, late.pop(0))
                assert not late
                for k in range(0, NBK, 2):
                    proj_x(g, k)
                    if k == 0:
                        softplus_exp(g)
                    if k == 2 * (LN_AFTER - 1):
                        softplus_ln(g)
                if g == G - 1:
                    prepare(0)
                    for p in range(PIECES):
                        split_hi(0, p)
                silu(g)
                if g + 1 < G:
                    norm_copy(xT, NT)

            act.wait_ge(par_in, 16)
            act.activation(par[:, C_A:C_A + NBK * NS], par[:, C_A:C_A + NBK * NS], ACT.Exp).then_inc(aexp, 1)
            act.wait_ge(ones_rdy, 1)
            norm_std(NT, mv1_, rstd1)
            norm_copy(xT, NT)
            attn_prep(0)
            attention_units(0)
            attn_end()
            projections(0)
            for g in range(G - 1):
                scan_decay(g, 0)
                scan_decay(g, 1)
                y_start(g)
                attn_prep(g + 1)
                attention_units(g + 1)
                for s in range(LEAD + NU + 2, min(NS, LEAD + NU + TAIL + 1)):
                    scan_decay(g, s)
                attn_end()
                projections(g + 1)
            scan_decay(G - 1, 0)
            scan_decay(G - 1, 1)
            y_start(G - 1)
            for j in range(-1, JOBS):
                if j >= 0 and j + 1 < JOBS and first_job(job(j + 1)[2]) == j + 1:
                    prepare(job(j + 1)[2])
                if j == -1:
                    gate_tanh(0)
                for k, p in splits(j):
                    split_hi(k, p)
                if 0 < j + 1 < JOBS:
                    gate_tanh(j + 1)
                if j == -1:
                    scan_decay(G - 1, 2)
                if j == OUT_JOB + 1:
                    norm_std(NT)
                for state, part in scan_parts(j):
                    if part == 1 and state + 2 < NS:
                        scan_decay(G - 1, state + 2)

        @block.vector
        def _(dve):
            jd, chain, norms, stats = Count(), Count(), Count(), Count()

            def step(ins):
                chain.n += 1
                ins.then_inc(dve_step, 1)
                dve.wait_ge(dve_step, chain.n)

            def job_d():
                jd.n += 1
                dve.wait_ge(d_full, jd.n)
                return bank[4 + (jd.n - 1) % 2]

            def norm_stats(tile0, n, var=mv_, std=rstd, first=0):
                for t in range(n):
                    step(dve.bn_stats(st_[:, 6 * t:6 * t + 6], xs[:, tile0 + t, :]))
                for t in range(n):
                    ins = dve.bn_aggr(var[:, 2 * (first + t):2 * (first + t) + 2], st_[:, 6 * t:6 * t + 6])
                stats.n += 1
                ins.then_inc(var_rdy, 1)
                dve.wait_ge(std_rdy, stats.n)
                step(dve.reciprocal(std[:, first:first + n], std[:, first:first + n]))

            def norm_apply(tile0, slot, var=mv_, std=rstd, first=0):
                for t in range(NT):
                    q = first + t
                    ins = dve.tensor_scalar(nrm[:, slot + t, :], xs[:, tile0 + t, :], var[:, 2 * q:2 * q + 1],
                                            std[:, q:q + 1], ALU.subtract, ALU.mult)
                norms.n += 1
                ins.then_inc(nrm_rdy, 1)
                dve.wait_ge(nrm_rdy, norms.n)

            def norm(tile0, slot):
                norm_stats(tile0, NT)
                norm_apply(tile0, slot)

            def key_bias(g):
                b = job_d()
                dve.wait_ge(bc_out, 16 * g) if g else None
                v = b[0:H, 0:GT].rearrange("p (u i) -> p u i", u=NU).unsqueeze(2).to_broadcast([H, NU, H, TI])
                m = ident[0:H, 0:H].unsqueeze(1).unsqueeze(3).to_broadcast([H, NU, H, TI])
                dve.tensor_tensor(sb8, v, m, ALU.mult).then_inc(d_free, 1)
                dve.wait_ge(d_free, jd.n)
                dve.nop().then_inc(sb8_rdy, 1)

            def neg_max(n):
                dve.wait_ge(s_full, n + 1)
                dve.tensor_reduce(nmax[:, n % 2 * QB:(n % 2 + 1) * QB],
                                  bank[n % 2][:, :].rearrange("p (b k) -> p b k", b=QB), AX_X, ALU.max,
                                  negate=True).then_inc(nm_rdy, 1)

            def add_tiles(g):
                for t in range(NT):
                    b = job_d()
                    tile = xs[:, g * NT + t, :]
                    dve.tensor_tensor(tile, tile, b[:, :], ALU.add).then_inc(d_free, 1)
                dve.wait_ge(d_free, jd.n)

            def conv(g, k0):
                n = g * NBK // 2 + k0 // 2
                dve.wait_ge(a_free, CONV_JOBS[g] + k0 // 2 + 1)
                for q in range(TAPS - 1):
                    for kk in range(2):
                        k = k0 + kk
                        v = u[g % 2][:, k, :].rearrange("p (b t) -> p b t", b=GB)
                        w = par[:, C_CW + k * TAPS + q:C_CW + k * TAPS + q + 1]
                        src = xi[n % 2][:, kk * GB:(kk + 1) * GB, q:q + T]
                        ins = dve.scalar_tensor_tensor(out=v, in0=src, scalar=w, in1=v, op0=ALU.mult, op1=ALU.add)
                    if q < TAPS - 2:
                        step(ins)
                ins.then_inc(conv_done, 1)

            def scan_inputs(g):
                d = del_s[g % 2]
                dve.wait_ge(sp_rdy, g + 1)
                step(dve.scalar_tensor_tensor(out=d, in0=d, scalar=0.0, in1=sp_tmp, op0=ALU.max, op1=ALU.add))
                dve.wait_ge(tanh_rdy, g + 1)
                step(dve.scalar_tensor_tensor(out=th_tmp, in0=th_tmp, scalar=1.0, in1=u_s[g % 2],
                                              op0=ALU.add, op1=ALU.mult))
                step(dve.scalar_tensor_tensor(out=u_s[g % 2], in0=th_tmp, scalar=0.5, in1=d,
                                              op0=ALU.mult, op1=ALU.mult))
                first = dlt[g % 2].rearrange("p k (b t) -> p (k b) t", t=T)[:, :, 0:1]
                dve.memset(first, RESET).then_inc(dl_rdy, 1)
                dve.wait_ge(dl_rdy, g + 1)

            def invert_sums(n):
                dve.wait_ge(p_exp, n + 1)
                rs = rsum[:, n % 2 * QB:(n % 2 + 1) * QB]
                dve.reciprocal(rs, rs).then_inc(sum_rdy, 1)

            def scan_step(g, j, parts=range(SCAN_PARTS)):
                n = g * NS + j
                h = hs_[:, :]
                h3 = h.rearrange("p (k t) -> p k t", k=NBK)
                bs, cs = (bcs[n % 2][:, w, :].unsqueeze(1).to_broadcast([P, NBK, GT]) for w in range(2))
                if 0 in parts:
                    dve.wait_ge(bc_in[n % 2], 16 * (n // 2 + 1))
                    step(dve.tensor_tensor(h3, u[g % 2], bs, ALU.mult))
                if 1 in parts:
                    dve.wait_ge(da_rdy, n + 1)
                    dve.tensor_tensor_scan(h, dA[n % 2], h, 0.0, ALU.mult, ALU.add).then_inc(scan_rd, 1)
                    dve.wait_ge(scan_rd, n + 1)
                if 2 in parts:
                    step(dve.tensor_tensor(h3, h3, cs, ALU.mult))
                if 3 in parts:
                    if j == 0:
                        dve.wait_ge(ys_rdy, g + 1)
                    dve.tensor_tensor(acc_[:, :], acc_[:, :], h, ALU.add).then_inc(step_done, 1)
                    dve.wait_ge(step_done, n + 1)

            def rank(out, v, n, tie):
                gt = rk1[:, 0:NT * n * n].rearrange("p (t i j) -> p t i j", t=NT, i=n)
                eq = rk2[:, 0:NT * n * n].rearrange("p (t i j) -> p t i j", t=NT, i=n)
                for t in range(NT):
                    mine = v[:, t, :].unsqueeze(2).to_broadcast([P, n, n])
                    other = v[:, t, :].unsqueeze(1).to_broadcast([P, n, n])
                    dve.tensor_tensor(gt[:, t], other, mine, ALU.is_gt)
                    ins = dve.tensor_tensor(eq[:, t], other, mine, ALU.is_equal)
                step(ins)
                ties = tie.unsqueeze(1).to_broadcast([P, NT, n * n])
                flat = [r[:, 0:NT * n * n].rearrange("p (t q) -> p t q", t=NT) for r in (rk1, rk2)]
                step(dve.tensor_tensor(flat[1], flat[1], ties, ALU.mult))
                step(dve.tensor_tensor(flat[0], flat[0], flat[1], ALU.add))
                step(dve.tensor_reduce(out, rk1[:, 0:NT * n * n].rearrange("p (r j) -> p r j", j=n), AX_X, ALU.add))

            def prepare_norm(c):
                if c == 1:
                    dve.wait_ge(bc_out, 16 * G)
                norm(c * NT, (c + 1) % 2 * NT)

            def prepare_input(c):
                n = x_item(first_job(c)) - 2
                dve.wait_ge(xt_rdy, c + 1)
                for k in range(2):
                    v = slice(k * 512, (k + 1) * 512)
                    ins = dve.tensor_tensor(xm[c % CA][1][:, v], X[n % 2][k][:, :], xm[c % CA][0][:, v], ALU.subtract)
                ins.then_inc(x_free, 1)
                dve.wait_ge(x_free, n + 1)
                dve.nop().then_inc(xm_rdy, 1)

            def free_logits(c):
                dve.wait_ge(lg_rdy, c + 1)
                dve.nop().then_inc(x_free, 1)

            def route(c):
                lg = lgs[c]
                tie4, tie16 = par[:, C_T4:C_T4 + NG * NG], par[:, C_T16:C_T16 + E * E]
                eb = par[:, C_EB:C_EB + E].unsqueeze(1).to_broadcast([P, NT, E])
                step(dve.tensor_scalar(sc, lg, 1.0, None, ALU.add))
                step(dve.reciprocal(sc, sc))
                tiles = lambda v: v.rearrange("p (t e) -> p t e", t=NT)
                step(dve.tensor_tensor(tiles(sfc), tiles(sc), eb, ALU.add))
                f = sfc.rearrange("p (r k) -> p r k", k=E // NG)
                m = [gs[:, k * NT * NG:(k + 1) * NT * NG] for k in range(4)]
                x0, x1, x2, x3 = (f[:, :, k] for k in range(4))
                dve.tensor_tensor(m[0], x0, x1, ALU.max)
                dve.tensor_tensor(m[1], x2, x3, ALU.max)
                dve.tensor_tensor(m[2], x0, x1, ALU.add)
                step(dve.tensor_tensor(m[3], x2, x3, ALU.add))
                step(dve.tensor_tensor(m[0], m[0], m[1], ALU.add))
                step(dve.tensor_tensor(m[2], m[2], m[3], ALU.max))
                step(dve.tensor_tensor(m[0], m[0], m[2], ALU.max))
                rank(m[1], tiles(m[0]), NG, tie4)
                step(dve.tensor_scalar(m[1], m[1], 2.0, None, ALU.is_lt))
                step(dve.tensor_tensor(f, f, m[1].unsqueeze(2).to_broadcast([P, NT * NG, E // NG]), ALU.mult))
                rank(lg, tiles(sfc), E, tie16)
                step(dve.tensor_scalar(lg, lg, float(TOPK), None, ALU.is_lt))
                step(dve.tensor_tensor(sc, sc, lg, ALU.mult))
                den = gs[:, 0:NT]
                step(dve.tensor_reduce(den, tiles(sc), AX_X, ALU.add))
                step(dve.tensor_scalar(den, den, 1e-20, None, ALU.add))
                step(dve.reciprocal(den, den))
                step(dve.tensor_scalar(den, den, 0.5, None, ALU.mult))
                step(dve.tensor_tensor(tiles(comb_[:, c * NT * E:(c + 1) * NT * E]), tiles(sc), den.unsqueeze(2).to_broadcast([P, NT, E]), ALU.mult))

            def split_lo(k, p):
                q = k * PIECES + p
                dve.wait_ge(w_hi_rdy, q + 1)
                hi, lo = (v[p].rearrange("p c i -> p (c i)") for v in w_gu[k % 2])
                dve.tensor_tensor(lo, raw[q % RAW], hi, ALU.subtract).then_inc(w_rdy, 1)

            def hidden(j):
                b = X[x_item(j) % 2]
                dve.wait_ge(th_rdy, j + 1)
                o = hid[j % 2]
                step(dve.scalar_tensor_tensor(out=o, in0=o, scalar=1.0, in1=b[0][:, :], op0=ALU.add, op1=ALU.mult))
                dve.tensor_tensor(o, o, b[1][:, :], ALU.mult).then_inc(x_free, 1)
                dve.wait_ge(x_free, x_item(j) + 1)
                dve.nop().then_inc(h_rdy, 1)

            def add_expert(j):
                k, e, c = job(j)
                n = y_item(j)
                dve.wait_ge(y_full, n + 1)
                for t in range(NT):
                    tile = xs[:, c * NT + t, :]
                    w = (c * NT + t) * E + e
                    ins = dve.scalar_tensor_tensor(out=tile, in0=Y[n % 2][t][:, :], scalar=comb_[:, w:w + 1],
                                                   in1=tile, op0=ALU.mult, op1=ALU.add)
                ins.then_inc(y_free, 1)
                dve.wait_ge(y_free, n + 1)

            def add_last_scan():
                n = y_item(OUT_JOB) - 1
                dve.wait_ge(y_full, n + 1)
                for t in range(NT):
                    tile = xs[:, CA * NT + t, :]
                    ins = dve.tensor_tensor(tile, tile, Y[n % 2][t][:, :], ALU.add)
                ins.then_inc(y_free, 1)
                dve.wait_ge(y_free, n + 1)

            dve.memset(epsc[:, :], EPS)
            dve.memset(ones8[:, :], 1.0).then_inc(ones_rdy, 1)
            for s in range(2):
                ins = dve.memset(xi[s][:, :, 0:TAPS - 1], 0.0)
            ins.then_inc(pad_rdy, 1)
            dve.wait_ge(par_in, 16)
            step(dve.tensor_scalar(par[:, C_BQ:C_BQ + DC], par[:, C_BQ:C_BQ + DC], DH ** -0.5, None, ALU.mult))
            step(dve.tensor_scalar(par[:, C_D:C_D + NBK], par[:, C_D:C_D + NBK], 0.5, None, ALU.mult))
            dve.wait_ge(aexp, 1)
            step(dve.tensor_scalar(par[:, C_A:C_A + NBK * NS], par[:, C_A:C_A + NBK * NS], -1.0, None, ALU.mult))
            dve.wait_ge(x_in, 16)
            norm_stats(0, NT, mv1_, rstd1)
            norm_apply(0, 0, mv1_, rstd1)
            key_bias(0)
            for k in range(NU):
                if k == STATS_UNIT:
                    dve.wait_ge(xr_in, 16)
                    norm_stats(NT, (G - 1) * NT, mv1_, rstd1, NT)
                neg_max(k)
                invert_sums(k)
            add_tiles(0)
            dve.nop().then_inc(x1_rdy, 1)
            norm(0, 0)
            norm_apply(NT, NT, mv1_, rstd1, NT)
            for k in range(0, NBK, 2):
                conv(0, k)
            scan_inputs(0)
            scan_step(0, 0, parts=(0, 1, 2))
            scan_step(0, 0, parts=(3,))
            for g in range(G - 1):
                for s in range(LEAD):
                    if s == LEAD - 2:
                        key_bias(g + 1)
                    if s > 0:
                        scan_step(g, s)
                for k in range(NU):
                    n = (g + 1) * NU + k
                    scan_step(g, LEAD + k, parts=(0,))
                    neg_max(n)
                    scan_step(g, LEAD + k, parts=(1,))
                    invert_sums(n)
                    scan_step(g, LEAD + k, parts=(2, 3))
                for s in range(TAIL):
                    scan_step(g, LEAD + NU + s)
                add_tiles(g + 1)
                dve.nop().then_inc(x1_rdy, 1)
                norm((g + 1) * NT, 0)
                if g + 2 < G:
                    norm_apply((g + 2) * NT, NT, mv1_, rstd1, (g + 2) * NT)
                else:
                    prepare_norm(0)
                late = list(range(LEAD + NU + TAIL, NS))
                for s in range(min(PRE, len(late))):
                    scan_step(g, late.pop(0))
                for k in range(0, NBK, 2):
                    conv(g + 1, k)
                    if late:
                        scan_step(g, late.pop(0))
                if g + 2 == G:
                    prepare_input(0)
                    prepare_norm(1)
                    for p in range(PIECES):
                        split_lo(0, p)
                    free_logits(0)
                scan_inputs(g + 1)
                scan_step(g + 1, 0, parts=(0, 1, 2))
                add_tiles(g)
                if g + 2 == G:
                    hidden(0)
                scan_step(g + 1, 0, parts=(3,))
            for j in range(-1, JOBS):
                if j >= 0 and j + 1 < JOBS and first_job(job(j + 1)[2]) == j + 1:
                    c = job(j + 1)[2]
                    prepare_input(c)
                    if c + 1 < CA:
                        prepare_norm(c + 1)
                    free_logits(c)
                for k, p in splits(j):
                    split_lo(k, p)
                if 0 < j + 1 < JOBS:
                    hidden(j + 1)
                if j - 1 == OUT_JOB:
                    add_last_scan()
                    prepare_norm(G - 1)
                if j >= 1:
                    if first_job(job(j - 1)[2]) == j - 1:
                        route(job(j - 1)[2])
                    add_expert(j - 1)
                if j - 1 == JA - 1:
                    dve.nop().then_inc(out_rdy, 1)
                for state, part in scan_parts(j):
                    scan_step(G - 1, state, parts=(part,))
            add_expert(JOBS - 1)
            dve.nop().then_inc(out_rdy, 1)


def kernel(**inputs):
    import numpy as np
    import concourse.bacc as bacc
    from concourse.bass_utils import run_bass_kernel_spmd

    a = {k: np.asarray(v) for k, v in inputs.items()}

    def cols(v, n):
        return v.reshape(n, P, -1).transpose(1, 0, 2).reshape(P, -1)

    bk = np.zeros((P, DC, H), np.float32)
    for m in range(DC):
        for hh in range(2):
            bk[hh * DH:(hh + 1) * DH, m, 2 * m + hh] = a["L0_xattn_bk"][m * P + hh * DH:m * P + (hh + 1) * DH]
    tie = [np.broadcast_to(np.tril(np.ones((n, n), np.float32), -1).reshape(1, -1), (P, n * n)) for n in (NG, E)]
    params = np.concatenate([
        cols(a["L0_xattn_bq"], DC), cols(a["L0_xattn_bv"], DC), cols(a["L0_attn_dt_proj_b"], NBK),
        cols(a["L0_attn_conv_w"], NBK), cols(a["L0_attn_conv_b"], NBK), cols(a["L0_attn_D"], NBK),
        cols(a["L0_attn_A_log"], NBK), bk.reshape(P, -1),
        np.broadcast_to(a["L0_ffn_e_bias"].reshape(1, -1), (P, E)), tie[0], tie[1], np.eye(P, dtype=np.float32)], axis=1)
    ctx = a["ctx_1024"]
    data = {
        "x": a["x"].reshape(G * GT, D),
        "ctx_t": ctx.reshape(NB, KEYS, 2, D).transpose(0, 2, 3, 1),
        "ctx_n": ctx,
        "wq_t": a["L0_xattn_Wq"].T, "wk": a["L0_xattn_Wk"], "wv_t": a["L0_xattn_Wv"].T,
        "xp_t": a["L0_attn_x_proj_w"].T, "dt_t": a["L0_attn_dt_proj_w"].T,
        "bc_t": np.concatenate([a["L0_attn_B_proj_w"], a["L0_attn_C_proj_w"]], axis=0).T,
        "ow_t": a["L0_attn_out_proj_w"].T, "gate_t": a["L0_ffn_gate_weight"].T,
        "eg_t": a["L0_ffn_gate_proj"].transpose(0, 2, 1), "eu_t": a["L0_ffn_up_proj"].transpose(0, 2, 1),
        "ed_t": a["L0_ffn_down_proj"].transpose(0, 2, 1),
        "params": params,
    }
    nc = bacc.Bacc("TRN2", target_bir_lowering=False, num_devices=1)
    arrays, args = {}, []
    for name, v in data.items():
        v = np.ascontiguousarray(v)
        arrays[f"in_{name}"] = v
        args.append(nc.dram_tensor(f"in_{name}", v.shape, F32, kind="ExternalInput").ap())
    args.append(nc.dram_tensor("bc_scratch", (G, 2 * NS, GT), F32, kind="Internal").ap())
    args.append(nc.dram_tensor("out_0", (G * GT, D), F32, kind="ExternalOutput").ap())
    perceiver_block(nc, *args)
    r = run_bass_kernel_spmd(nc, [arrays], core_ids=[0])
    return r.results[0]["out_0"].reshape(NB, T, D)
```
